# Optimizing a Trainium2 kernel written in Bass

```python
import numpy as np
import jax
import jax.numpy as jnp

def _softmax(x, axis=-1):
    return jax.nn.softmax(x, axis=axis)

def _gelu(x):
    return jax.nn.gelu(x, approximate=True)

def _silu(x):
    return jax.nn.silu(x)

def _sigmoid(x):
    return jax.nn.sigmoid(x)

def _layernorm(x, axis=-1, eps=1e-05):
    m = jnp.mean(x, axis=axis, keepdims=True)
    v = jnp.var(x, axis=axis, keepdims=True)
    return (x - m) / jnp.sqrt(v + eps)

def _scatter_add(tgt, idx, src, axis=0):
    return tgt.at[idx].add(src)

def _segment_sum(src, seg, n):
    return jax.ops.segment_sum(src, seg, n)
kernel_name = 'mk_gnn_preln_d1_gnn_r64_586c95'

def setup_inputs(seed: int=0):
    np.random.seed(seed)
    _w = jnp.asarray

    def _rec_inputs():
        import jax
        import jax.numpy as jnp
        _gk = jax.random.key(seed)
        x = -0.0009044 + 1 * jax.random.normal(jax.random.fold_in(_gk, 1), (100000, 160), jnp.float32)
        src = jax.random.randint(jax.random.fold_in(_gk, 2), (25000,), 0, 100000, jnp.int32)
        dst = jnp.minimum((100000 * jax.random.uniform(jax.random.fold_in(_gk, 3), (25000,)) ** 2.0).astype(jnp.int32), 99999)
        _o = jnp.argsort(dst, stable=True)
        src = src[_o]
        dst = dst[_o]
        edge_attr_3 = 0.00047201 + 1.00023 * jax.random.normal(jax.random.fold_in(_gk, 11), (25000, 3), jnp.float32)
        edge_attr_64 = 0.000279952 + 1.00013 * jax.random.normal(jax.random.fold_in(_gk, 12), (25000, 64), jnp.float32)
        return (x, src, dst, edge_attr_3, edge_attr_64)
    x, src, dst, edge_attr_3, edge_attr_64 = _rec_inputs()

    def _L0_gnn_setup():
        import jax, jax.numpy as jnp
        import numpy as np
        N_NODES = 10000
        N_EDGES = 5000
        MUL0, MUL1 = (64, 32)
        EDGE_DIM = 64
        W_NUMEL = 224
        DENOM = 32.0
        SQRT3 = 3.0 ** 0.5
        INV_SQRT3 = 1.0 / SQRT3
        INV_SQRT2 = 2.0 ** (-0.5)

        def _forward(node_feature, edge_attr, edge_feature, W_skip0, W_skip1, W_nl0, W_nl1, W_fc1, W_fc2, W_out_s, W_out_v, edge_index):
            N = node_feature.shape[0]
            E = edge_attr.shape[0]
            s = node_feature[:, :MUL0]
            v = node_feature[:, MUL0:].reshape(N, MUL1, 3)
            skip_s = s @ W_skip0
            skip_v = jnp.einsum('nmi,mk->nki', v, W_skip1)
            s = s @ W_nl0
            v = jnp.einsum('nmi,mk->nki', v, W_nl1)
            rhat = edge_attr / jnp.linalg.norm(edge_attr, axis=-1, keepdims=True)
            sh1 = SQRT3 * rhat
            w = jax.nn.relu(edge_feature @ W_fc1) @ W_fc2
            w0, w1, w2, w3, w4 = jnp.split(w, [64, 128, 160, 192], axis=-1)
            src, dst = (edge_index[0], edge_index[1])
            xs = s[dst]
            xv = v[dst]
            out0a = w0 * xs
            out0b = w3 * (jnp.einsum('emi,ei->em', xv, sh1) * INV_SQRT3)
            out1a = (w1 * xs)[:, :, None] * sh1[:, None, :]
            out1b = w2[:, :, None] * xv
            out1c = w4[:, :, None] * (jnp.cross(xv, sh1[:, None, :]) * INV_SQRT2)
            tp = jnp.concatenate([out0a, out0b, out1a.reshape(E, -1), out1b.reshape(E, -1), out1c.reshape(E, -1)], axis=-1)
            agg = jax.ops.segment_sum(tp, src, num_segments=N) / DENOM
            agg_s = agg[:, :96]
            agg_v = agg[:, 96:].reshape(N, 128, 3)
            out_s = agg_s @ W_out_s + skip_s
            out_v = jnp.einsum('nmi,mk->nki', agg_v, W_out_v) + skip_v
            fs = jax.nn.silu(out_s[:, :MUL0])
            gate = jax.nn.sigmoid(out_s[:, MUL0:MUL0 + 32])
            gv = gate[:, :, None] * out_v
            return jnp.concatenate([fs, gv.reshape(N, -1)], axis=-1)
        key = jax.random.key(seed)
        ks = jax.random.split(key, 12)

        def lin(k, fi, fo):
            return jax.random.normal(k, (fi, fo), jnp.float32) / np.float32(np.sqrt(fi))
        return {'node_feature': jax.random.normal(ks[0], (N_NODES, MUL0 + 3 * MUL1), jnp.float32), 'edge_attr': jax.random.normal(ks[1], (N_EDGES, 3), jnp.float32), 'edge_feature': jax.random.normal(ks[2], (N_EDGES, EDGE_DIM), jnp.float32), 'W_skip0': lin(ks[3], MUL0, 96), 'W_skip1': lin(ks[4], MUL1, 32), 'W_nl0': lin(ks[5], MUL0, MUL0), 'W_nl1': lin(ks[6], MUL1, MUL1), 'W_fc1': lin(ks[7], EDGE_DIM, 64), 'W_fc2': lin(ks[8], 64, W_NUMEL), 'W_out_s': lin(ks[9], 96, 96), 'W_out_v': lin(ks[10], 128, 32), 'edge_index': jax.random.randint(ks[11], (2, N_EDGES), 0, N_NODES)}
    _L0_gnn_all = _L0_gnn_setup()
    _L0_gnn_in = {k: v for k, v in _L0_gnn_all.items() if k in ('W_skip0', 'W_skip1', 'W_nl0', 'W_nl1', 'W_fc1', 'W_fc2', 'W_out_s', 'W_out_v')}
    del _L0_gnn_all
    return {'x': x, 'src': src, 'dst': dst, 'edge_attr_3': edge_attr_3, 'edge_attr_64': edge_attr_64, 'L0_gnn_W_skip0': _L0_gnn_in['W_skip0'], 'L0_gnn_W_skip1': _L0_gnn_in['W_skip1'], 'L0_gnn_W_nl0': _L0_gnn_in['W_nl0'], 'L0_gnn_W_nl1': _L0_gnn_in['W_nl1'], 'L0_gnn_W_fc1': _L0_gnn_in['W_fc1'], 'L0_gnn_W_fc2': _L0_gnn_in['W_fc2'], 'L0_gnn_W_out_s': _L0_gnn_in['W_out_s'], 'L0_gnn_W_out_v': _L0_gnn_in['W_out_v']}

def reference(x, src, dst, edge_attr_3, edge_attr_64, L0_gnn_W_skip0, L0_gnn_W_skip1, L0_gnn_W_nl0, L0_gnn_W_nl1, L0_gnn_W_fc1, L0_gnn_W_fc2, L0_gnn_W_out_s, L0_gnn_W_out_v):
    import jax
    import jax.numpy as jnp

    def _L0_gnn_ref(node_feature, edge_attr, edge_feature, W_skip0, W_skip1, W_nl0, W_nl1, W_fc1, W_fc2, W_out_s, W_out_v, edge_index):
        import jax, jax.numpy as jnp
        import numpy as np
        N_NODES = 10000
        N_EDGES = 5000
        MUL0, MUL1 = (64, 32)
        EDGE_DIM = 64
        W_NUMEL = 224
        DENOM = 32.0
        SQRT3 = 3.0 ** 0.5
        INV_SQRT3 = 1.0 / SQRT3
        INV_SQRT2 = 2.0 ** (-0.5)

        def _forward(node_feature, edge_attr, edge_feature, W_skip0, W_skip1, W_nl0, W_nl1, W_fc1, W_fc2, W_out_s, W_out_v, edge_index):
            N = node_feature.shape[0]
            E = edge_attr.shape[0]
            s = node_feature[:, :MUL0]
            v = node_feature[:, MUL0:].reshape(N, MUL1, 3)
            skip_s = s @ W_skip0
            skip_v = jnp.einsum('nmi,mk->nki', v, W_skip1)
            s = s @ W_nl0
            v = jnp.einsum('nmi,mk->nki', v, W_nl1)
            rhat = edge_attr / jnp.linalg.norm(edge_attr, axis=-1, keepdims=True)
            sh1 = SQRT3 * rhat
            w = jax.nn.relu(edge_feature @ W_fc1) @ W_fc2
            w0, w1, w2, w3, w4 = jnp.split(w, [64, 128, 160, 192], axis=-1)
            src, dst = (edge_index[0], edge_index[1])
            xs = s[dst]
            xv = v[dst]
            out0a = w0 * xs
            out0b = w3 * (jnp.einsum('emi,ei->em', xv, sh1) * INV_SQRT3)
            out1a = (w1 * xs)[:, :, None] * sh1[:, None, :]
            out1b = w2[:, :, None] * xv
            out1c = w4[:, :, None] * (jnp.cross(xv, sh1[:, None, :]) * INV_SQRT2)
            tp = jnp.concatenate([out0a, out0b, out1a.reshape(E, -1), out1b.reshape(E, -1), out1c.reshape(E, -1)], axis=-1)
            agg = jax.ops.segment_sum(tp, src, num_segments=N) / DENOM
            agg_s = agg[:, :96]
            agg_v = agg[:, 96:].reshape(N, 128, 3)
            out_s = agg_s @ W_out_s + skip_s
            out_v = jnp.einsum('nmi,mk->nki', agg_v, W_out_v) + skip_v
            fs = jax.nn.silu(out_s[:, :MUL0])
            gate = jax.nn.sigmoid(out_s[:, MUL0:MUL0 + 32])
            gv = gate[:, :, None] * out_v
            return jnp.concatenate([fs, gv.reshape(N, -1)], axis=-1)
        return _forward(node_feature, edge_attr, edge_feature, W_skip0, W_skip1, W_nl0, W_nl1, W_fc1, W_fc2, W_out_s, W_out_v, edge_index)
    edge_index = jnp.stack([src, dst])
    h = jnp.maximum(_layernorm(x, axis=-1), 0.0)
    x = x + _L0_gnn_ref(h, edge_attr_3, edge_attr_64, L0_gnn_W_skip0, L0_gnn_W_skip1, L0_gnn_W_nl0, L0_gnn_W_nl1, L0_gnn_W_fc1, L0_gnn_W_fc2, L0_gnn_W_out_s, L0_gnn_W_out_v, edge_index)
    return x

_drawn_inputs = setup_inputs


def setup_inputs(seed=0):
    import zlib

    import numpy as np

    out = dict(_drawn_inputs(seed))
    spreads = {}
    factors = {'edge_attr_3': 8.0,
     'edge_attr_64': 8.0,
     'L0_gnn_W_nl0': 8.0,
     'L0_gnn_W_nl1': 8.0,
     'L0_gnn_W_fc1': 8.0,
     'L0_gnn_W_fc2': 8.0,
     'L0_gnn_W_out_s': 8.0,
     'L0_gnn_W_out_v': 8.0,
     'L0_gnn_W_skip0': 7.02,
     'L0_gnn_W_skip1': 28.875}
    for name, (base, spread) in spreads.items():
        noise = np.random.default_rng([zlib.crc32(name.encode()), seed]).standard_normal(out[name].shape)
        drawn = base * np.exp(spread * noise) if base else spread * noise
        out[name] = jnp.asarray(drawn.astype(out[name].dtype))
    for name, factor in factors.items():
        out[name] = (out[name] * factor).astype(out[name].dtype)
    return out
```

```python
from contextlib import ExitStack

import concourse.bass as bass
from concourse import mybir

ALU = mybir.AluOpType
ACT = mybir.ActivationFunctionType
F32 = mybir.dt.float32
F16 = mybir.dt.float16
BF16 = mybir.dt.bfloat16
I32 = mybir.dt.int32
AX_X = mybir.AxisListType.X

P = 128
EPS = 1e-5


def gnn_layer(nc, x, src, dst, edge_vec, edge_feat_t, w_skip0, w_skip1, w_nl0, w_nl1,
              w_fc1, w_fc2, w_out_s, w_out_v, out):
    N, F = x.shape
    S = w_skip0.shape[0]
    V = w_skip1.shape[0]
    SG = w_skip0.shape[1]
    W = w_fc2.shape[1]
    Z = SG + 3 * V
    assert (S, V, F, SG, W) == (64, 32, 160, 96, 224)

    ET, NT = src.shape
    GE = 4
    NG = NT // GE
    EF = edge_feat_t.shape[0]
    assert NT % GE == 0 and NG % 2 == 0

    G = 8
    MN = P * G
    NM = -(-N // MN)
    LAST_P = (N - (NM - 1) * MN) // G
    assert N % G == 0
    BPM = G // 2
    NB = NM * BPM
    CAP = P
    MW = 200
    LOCAL, NODE = Z, Z + 1
    CORE = GE * 64
    TS = 256

    messages = nc.dram_tensor("messages", (1 + ET * NT, MW), F32).ap()

    with ExitStack() as ctx:
        def sb(name, shape, dt=F32):
            return ctx.enter_context(nc.sbuf_tensor(name, shape, dt))

        def sem(name):
            return ctx.enter_context(nc.semaphore(name))

        ident = sb("ident", [P, P])
        tri_before = sb("tri_before", [ET, ET], BF16)
        tri_rest = sb("tri_rest", [ET, ET], BF16)
        iota_i = sb("iota_i", [P, 512], I32)
        iota_bin = sb("iota_bin", [P, NB], F16)
        iota_slot = sb("iota_slot", [P, CAP], F16)
        iota_local = sb("iota_local", [P, 2 * P])
        zeros_bf = sb("zeros_bf", [P, NB], BF16)
        neg_half = sb("neg_half", [P, G])
        src_i = sb("src_i", [ET, NT], I32)
        dst_i = sb("dst_i", [ET, NT], I32)
        num_i = sb("num_i", [ET, NT], I32)
        tmp_a = sb("tmp_a", [ET, NT], I32)
        tmp_b = sb("tmp_b", [ET, NT], I32)
        bin_of = sb("bin_of", [ET, NT])
        place_of = sb("place_of", [ET, NT, 2])
        num_hi = sb("num_hi", [ET, NT])
        num_lo = sb("num_lo", [ET, NT])
        vec = sb("vec", [ET, NT, 3])
        vec_sq = sb("vec_sq", [ET, NT, 3])
        vec_d2 = sb("vec_d2", [ET, NT])
        vec_r = sb("vec_r", [ET, NT])
        half_nt = sb("half_nt", [ET, NT])
        hat = sb("hat", [ET, NT, 4])
        slots_i = sb("slots_i", [CAP, NB], I32)
        tab_lo = sb("tab_lo", [CAP, NB])
        most = sb("most", [ET, 1])
        most_i = sb("most_i", [ET, 1], I32)

        wsk_a = sb("wsk_a", [P, SG + 2 * V])
        wsk_z = sb("wsk_z", [P, 4 * V])
        wnl_a = sb("wnl_a", [P, S + 2 * V])
        wnl_z = sb("wnl_z", [P, 4 * V])
        wfc1 = sb("wfc1", [EF, P])
        wfc2 = sb("wfc2", [EF, W])
        wos = sb("wos", [SG, SG])
        wov = sb("wov", [P, V])

        bin_hot = sb("bin_hot", [ET, GE, NB], BF16)
        rank_junk = sb("rank_junk", [ET, NB])
        rank = sb("rank", [ET, GE])
        slot_hi = sb("slot_hi", [ET, GE, CAP], BF16)
        slot_lo = sb("slot_lo", [ET, GE, CAP], BF16)

        dst_g = sb("dst_g", [ET, 2, GE], I32)
        xg = sb("xg", [ET, 2, GE, F])
        ef = sb("ef", [EF, 2, GE * ET])
        e_stat = sb("e_stat", [ET, 2, GE, 6])
        e_sum = sb("e_sum", [ET, 2, 5, GE])
        e_rstd = sb("e_rstd", [ET, 2, GE])
        e_bias = sb("e_bias", [ET, 2, GE])
        hn = sb("hn", [ET, 2, F, GE])
        ht = sb("ht", [P, GE * ET])
        hz = sb("hz", [P, ET])
        hid = sb("hid", [EF, GE * ET])
        w_sb = sb("w_sb", [ET, 2, GE, W])
        tp_s = sb("tp_s", [ET, GE, P])
        tp_v = sb("tp_v", [ET, GE, 3, P])
        w1xs = sb("w1xs", [ET, GE, S])
        xvh = sb("xvh", [ET, GE, 3, V])
        dot = sb("dot", [ET, 2, GE, V])
        w4xv = sb("w4xv", [ET, GE, 3, V])
        cr_a = sb("cr_a", [ET, GE, 3, V])
        cr_b = sb("cr_b", [ET, GE, 3, V])
        tpt = sb("tpt", [P, 2, 4 * ET])
        msg = sb("msg", [ET, 2, GE, MW])
        row0 = sb("row0", [1, MW])

        RC = 10
        NC = NT // RC
        CREDIT = 2 * RC
        again = sb("again", [ET, 2, RC, MW])
        rel = sb("rel", [ET, 2, RC])
        macro_base = sb("macro_base", [ET, 1])
        iota_key = sb("iota_key", [ET, MN])
        key_hot = sb("key_hot", [ET, 2, MN])
        zeros_w = sb("zeros_w", [ET, P])

        U = 3
        xb = sb("xb", [P, U, G, F])
        n_stat = sb("n_stat", [P, U, G, 6])
        n_sum = sb("n_sum", [P, U, 5, G])
        n_rstd = sb("n_rstd", [P, U, G])
        n_bias = sb("n_bias", [P, U, G])
        nn = sb("nn", [P, U, 2, F, 4])
        slot_m = sb("slot_m", [P, U, BPM], I32)
        mg = sb("mg", [P, U, BPM, MW])
        hot = sb("hot", [P, U, BPM, 2 * P])
        nt_a = sb("nt_a", [P, 2, 4 * P])
        nt_z = sb("nt_z", [P, 2, P])
        sg = sb("sg", [P, 2, 4, SG])
        ob = sb("ob", [P, U, G, F])

        s_in = sem("s_in")
        s_w = sem("s_w")
        s_clr = sem("s_clr")
        s_const = sem("s_const")
        s_pc = sem("s_pc")
        s_dc = sem("s_dc")
        s_tab = sem("s_tab")
        s_r = sem("s_r")
        s_wready = sem("s_wready")
        s_row0 = sem("s_row0")
        s_held = sem("s_held")

        b_hot = sem("b_hot")
        b_pre = sem("b_pre")
        b_rank = sem("b_rank")
        b_slot = sem("b_slot")
        b_tab = sem("b_tab")
        b_lo = sem("b_lo")
        b_most = sem("b_most")
        b_end = sem("b_end")
        b_fin = sem("b_fin")

        e_idx = sem("e_idx")
        e_x = [sem("e_x0"), sem("e_x1")]
        e_f = [sem("e_f0"), sem("e_f1")]
        e_c2 = sem("e_c2")
        e_c3 = sem("e_c3")
        e_c = sem("e_c")
        e_var = sem("e_var")
        e_pw = sem("e_pw")
        e_ln = sem("e_ln")
        e_norm = sem("e_norm")
        e_t = sem("e_t")
        e_ht = sem("e_ht")
        e_h1 = sem("e_h1")
        e_hid = sem("e_hid")
        e_w = sem("e_w")
        e_wsb = sem("e_wsb")
        e_xs = sem("e_xs")
        e_px = sem("e_px")
        e_t1 = sem("e_t1")
        e_gp = sem("e_gp")
        e_tp = sem("e_tp")
        e_tt = sem("e_tt")
        e_ttsb = sem("e_ttsb")
        e_m = sem("e_m")
        e_msb = sem("e_msb")
        e_loc = sem("e_loc")
        e_st = [sem("e_st0"), sem("e_st1")]

        class Nodes:

            def __init__(self, name):
                self.x = [sem(f"{name}_x{u}") for u in range(U)]
                self.idx = sem(f"{name}_idx")
                self.g = [sem(f"{name}_g{u}") for u in range(U)]
                self.c = sem(f"{name}_c")
                self.var = sem(f"{name}_var")
                self.pw = sem(f"{name}_pw")
                self.ln = sem(f"{name}_ln")
                self.norm = sem(f"{name}_norm")
                self.t = sem(f"{name}_t")
                self.ht = sem(f"{name}_ht")
                self.hot = sem(f"{name}_hot")
                self.z = sem(f"{name}_z")
                self.sg = sem(f"{name}_sg")
                self.mul = sem(f"{name}_mul")
                self.res = sem(f"{name}_res")
                self.st = [sem(f"{name}_st{u}") for u in range(U)]

        main = Nodes("n")
        redo = Nodes("r")
        r_iota = sem("r_iota")
        r_key = sem("r_key")
        r_m = [sem("r_m0"), sem("r_m1")]
        r_rel = sem("r_rel")
        r_base = sem("r_base")
        r_used = sem("r_used")

        def wait(eng, s, value):
            if not (isinstance(value, int) and value <= 0):
                eng.wait_ge(s, value)

        def groups(eng, body):
            body(0, 0, True, False)
            body(1, 1, True, True)
            body(2, 0, True, True)
            with eng.Fori(0, NG // 2 - 2) as r:
                body(2 * r + 3, 1, True, True)
                body(2 * r + 4, 0, True, True)
            body(NG - 1, 1, True, True)
            body(NG, 0, False, True)

        def chunks(eng, body):
            with eng.Fori(0, NC // 2) as r:
                body(2 * r, 0)
                body(2 * r + 1, 1)

        def macros(eng, body):
            for i in range(U):
                body(i, i % U)
            full = (NM - 3 - U) // U
            with eng.Fori(0, full) as r:
                for u in range(U):
                    body(U + U * r + u, u)
            for i in range(U + U * full, NM):
                body(i, i % U)

        with ExitStack() as psum_ctx:
            def ps(name, shape, dt=F32):
                return psum_ctx.enter_context(nc.psum_tensor(name, shape, dt))

            bank = [ps(f"bank{i}", [P, 1024]) for i in range(4)]

            p_cnt = bank[0][0:ET, 0:NB]
            p_hi = bank[1][:, 0:NB]
            p_lo = bank[2][:, 0:NB]
            p_t = bank[0][:, 0:GE * ET]
            p_tz = bank[0][:, 512:512 + ET]
            p_w = bank[1][0:ET, :].rearrange("p (t c) -> p t c", c=TS)[:, :, 0:W]
            p_x = bank[2][0:ET, :].rearrange("p (t c) -> p t c", c=TS)[:, :, 0:F]
            p_xs = p_x[:, :, 0:S]
            p_xv = p_x[:, :, S:F].rearrange("p t (i k) -> p t i k", i=3)
            p_h = bank[3][:, 0:GE * ET]
            p_m = bank[3][0:ET, 0:2 * Z].rearrange("p (t c) -> p t c", c=Z)
            p_tt = bank[3][:, 512:512 + 4 * ET]
            q_t = [bank[0][:, 0:512], bank[0][:, 512:1024]]
            q_tz = [bank[1][:, 0:P], bank[1][:, 512:512 + P]]
            q_z = [bank[2 + h][:, :].rearrange("p (t c) -> p t c", c=TS) for h in range(2)]

            block = psum_ctx.enter_context(nc.Block())

            @block.sync
            def _(sp):
                sp.dma_start(src_i[:], src).then_inc(s_in, 16)
                sp.dma_start(dst_i[:], dst).then_inc(s_in, 16)
                sp.dma_start(vec[:], edge_vec).then_inc(s_in, 16)
                sp.dma_start(wfc2[:], w_fc2).then_inc(s_w, 16)
                sp.dma_start(wos[:], w_out_s).then_inc(s_w, 16)
                sp.dma_start(wov[:], w_out_v).then_inc(s_w, 16)
                sp.wait_ge(s_clr, 1)
                sp.dma_start(wfc1[:, 0:EF], w_fc1).then_inc(s_w, 16)
                sp.dma_start(wsk_a[0:S, 0:SG], w_skip0).then_inc(s_w, 16)
                sp.dma_start(wnl_a[0:S, 0:S], w_nl0).then_inc(s_w, 16)
                for j in range(2):
                    rows = slice(S + V * j, S + V * j + V)
                    sp.dma_start(wsk_a[rows, SG + V * j:SG + V * j + V], w_skip1).then_inc(s_w, 16)
                    sp.dma_start(wnl_a[rows, S + V * j:S + V * j + V], w_nl1).then_inc(s_w, 16)
                for j in range(4):
                    cols = slice(V * j, V * j + V)
                    sp.dma_start(wsk_z[j:P:4, cols], w_skip1).then_inc(s_w, 16)
                    sp.dma_start(wnl_z[j:P:4, cols], w_nl1).then_inc(s_w, 16)
                sp.dma_start(messages[0:1, :], row0[:, :]).then_inc(s_row0, 16)

                def store_msgs(p, b):
                    sp.wait_ge(e_msb, 2 * p + 2)
                    sp.wait_ge(e_loc, p + 1)
                    rows = messages[bass.ds(p * (GE * ET) + 1, GE * ET), :]
                    sp.dma_start(rows.rearrange("(t p) c -> p t c", p=ET), msg[:, b, :, :]).then_inc(e_st[b], 16)

                def round_e(q, b, front, back):
                    if front:
                        wait(sp, e_h1, q - 1)
                        sp.dma_start(ef[:, b, :], edge_feat_t[:, bass.ds(q * (GE * ET), GE * ET)]).then_inc(e_f[b], 16)
                    if back:
                        store_msgs(q - 1, 1 - b)

                groups(sp, round_e)

                def nodes(n, every):
                    def load_x(i, u):
                        rows = x[bass.ds(i * MN, MN), :].rearrange("(p g) f -> p g f", g=G)
                        sp.dma_start(xb[:, u, :, :], rows).then_inc(n.x[u], 16)

                    def load_last(u):
                        rows = x[(NM - 1) * MN:N, :].rearrange("(p g) f -> p g f", g=G)
                        sp.dma_start(xb[0:LAST_P, u, :, :], rows).then_inc(n.x[u], 16)

                    def store_o(i, u):
                        sp.wait_ge(n.res, i + 1)
                        if isinstance(i, int) and i == NM - 1:
                            rows = out[(NM - 1) * MN:N, :].rearrange("(p g) f -> p g f", g=G)
                            sp.dma_start(rows, ob[0:LAST_P, u, :, :]).then_inc(n.st[u], 16)
                        else:
                            rows = out[bass.ds(i * MN, MN), :].rearrange("(p g) f -> p g f", g=G)
                            sp.dma_start(rows, ob[:, u, :, :]).then_inc(n.st[u], 16)

                    load_x(0, 0)
                    load_x(1, 1)

                    def round_n(i, u):
                        if isinstance(i, int):
                            if i >= 1:
                                store_o(i - 1, (u + 2) % U)
                            if i + 2 < NM - 1:
                                load_x(i + 2, (u + 2) % U)
                            elif i + 2 == NM - 1:
                                load_last((u + 2) % U)
                        else:
                            store_o(i - 1, (u + 2) % U)
                            load_x(i + 2, (u + 2) % U)
                        if every:
                            def chunk(k, b):
                                sp.wait_ge(r_used, RC * (i * NC + k - 1) + CREDIT)
                                rows = messages[bass.ds(k * (RC * ET) + 1, RC * ET), :]
                                sp.dma_start(again[:, b, :, :], rows.rearrange("(t p) c -> p t c", p=ET)
                                             ).then_inc(r_m[b], 16)

                            chunks(sp, chunk)

                    macros(sp, round_n)
                    store_o(NM - 1, (NM - 1) % U)
                    for u in range(U):
                        sp.wait_ge(n.st[u], 16 * len(range(u, NM, U)))

                nodes(main, False)
                sp.wait_ge(b_fin, 1)
                with sp.If(sp.value_load(most_i[0:1, 0:1]) > CAP):
                    nodes(redo, True)

            @block.gpsimd
            def _(pool):
                pool.memset(neg_half[:], -0.5).then_inc(s_const, 1)
                pool.memset(half_nt[:], -0.5).then_inc(s_const, 1)
                pool.memset(ident[:], 0.0).then_inc(s_pc, 1)
                pool.memset(tri_before[:], 0.0).then_inc(s_pc, 1)
                pool.memset(tri_rest[:], 0.0).then_inc(s_pc, 1)
                pool.iota(iota_i[:], pattern=[[1, 512]], base=0, channel_multiplier=0).then_inc(s_const, 1)
                pool.iota(num_i[:], pattern=[[ET, NT]], base=1, channel_multiplier=1).then_inc(s_const, 1)
                pool.wait_ge(s_pc, 3)
                pool.affine_select(out=ident[:], in_=ident[:], compare_op=ALU.not_equal, fill=1.0, base=0,
                                   pattern=[[-1, P]], channel_multiplier=1).then_inc(s_const, 1)
                pool.affine_select(out=tri_before[:], in_=tri_before[:], compare_op=ALU.is_ge, fill=1.0, base=0,
                                   pattern=[[-1, ET]], channel_multiplier=1).then_inc(s_const, 1)
                pool.affine_select(out=tri_rest[:], in_=tri_rest[:], compare_op=ALU.is_gt, fill=1.0, base=0,
                                   pattern=[[1, ET]], channel_multiplier=-1).then_inc(s_const, 1)
                pool.wait_ge(s_const, 7)
                pool.wait_ge(s_tab, 1)
                pool.tensor_tensor(vec_r[:], vec_d2[:], half_nt[:], ALU.pow).then_inc(s_r, 1)

                def gathers(q, b):
                    wait(pool, e_norm, q - 1)
                    pool.tensor_copy(dst_g[:, b, :], dst_i[:, bass.ds(q * GE, GE)]).then_inc(e_idx, 1)
                    pool.wait_ge(e_idx, q + 1)
                    pool.sem_inc(s_held, 1)
                    for t in range(GE):
                        pool.indirect_dma_start(xg[:, b, t, :], None, x[:, :],
                                                bass.IndirectOffsetOnAxis(ap=dst_g[:, b, t:t + 1], axis=0)
                                                ).then_inc(e_x[b], 16)

                pool.wait_ge(s_in, 48)
                gathers(0, 0)

                def round_e(q, b, front, back):
                    last = isinstance(q, int) and q + 1 >= NG
                    if front and not last:
                        gathers(q + 1, 1 - b)
                    if front:
                        pool.wait_ge(e_var, q + 1)
                        pool.tensor_tensor(e_rstd[:, b, :], e_sum[:, b, 4, :], neg_half[0:ET, 0:GE], ALU.pow).then_inc(e_pw, 1)
                        pool.wait_ge(e_pw, q + 1)
                        pool.tensor_tensor(e_bias[:, b, :], e_sum[:, b, 2, :], e_rstd[:, b, :], ALU.mult).then_inc(e_ln, 1)
                    if back:
                        p, c = q - 1, 1 - b
                        h = hat[:, bass.ds(p * GE, GE), :]
                        pool.wait_ge(e_t1, p + 1)
                        pool.tensor_tensor(tp_v[:, :, :, 0:S],
                                           w1xs[:, :, :].unsqueeze(2).to_broadcast((ET, GE, 3, S)),
                                           h[:, :, 0:3].unsqueeze(3).to_broadcast((ET, GE, 3, S)), ALU.mult)
                        pool.tensor_tensor(cr_a[:, :, 0:2, :], w4xv[:, :, 1:3, :],
                                           h[:, :, 2:4].unsqueeze(3).to_broadcast((ET, GE, 2, V)), ALU.mult)
                        pool.tensor_tensor(cr_a[:, :, 2, :], w4xv[:, :, 0, :],
                                           h[:, :, 1:2].to_broadcast((ET, GE, V)), ALU.mult).then_inc(e_gp, 1)

                groups(pool, round_e)

                def nodes(n, every):
                    def fetch(i, u):
                        wait(pool, n.z, 2 * (i - 2))
                        pool.tensor_copy(slot_m[:, u, :], slots_i[:, bass.ds(i * BPM, BPM)]).then_inc(n.idx, 1)
                        pool.wait_ge(n.idx, i + 1)
                        pool.sem_inc(s_held, 1)
                        for k in range(BPM):
                            pool.indirect_dma_start(mg[:, u, k, :], None, messages[:, :],
                                                    bass.IndirectOffsetOnAxis(ap=slot_m[:, u, k:k + 1], axis=0)
                                                    ).then_inc(n.g[u], 16)

                    def ln_n(i, u):
                        pool.wait_ge(n.var, i + 1)
                        pool.tensor_tensor(n_rstd[:, u, :], n_sum[:, u, 4, :], neg_half[:, :], ALU.pow).then_inc(n.pw, 1)
                        pool.wait_ge(n.pw, i + 1)
                        pool.tensor_tensor(n_bias[:, u, :], n_sum[:, u, 2, :], n_rstd[:, u, :], ALU.mult).then_inc(n.ln, 1)

                    if not every:
                        fetch(0, 0)
                    ln_n(0, 0)

                    def round_n(i, u):
                        if not (isinstance(i, int) and i + 1 >= NM):
                            if not every:
                                fetch(i + 1, (u + 1) % U)
                            ln_n(i + 1, (u + 1) % U)
                        pool.wait_ge(n.mul, 2 * i + 2)
                        pool.tensor_tensor(ob[:, u, :, :], ob[:, u, :, :], xb[:, u, :, :], ALU.add).then_inc(n.res, 1)

                    macros(pool, round_n)

                pool.wait_ge(b_fin, 1)
                pool.wait_ge(s_row0, 16)
                pool.wait_ge(e_st[0], 16 * (NG // 2))
                pool.wait_ge(e_st[1], 16 * (NG // 2))
                nodes(main, False)
                pool.wait_ge(b_fin, 1)
                with pool.If(pool.value_load(most_i[0:1, 0:1]) > CAP):
                    pool.iota(iota_i[:], pattern=[[1, 4], [G, P]], base=0, channel_multiplier=0).then_inc(r_iota, 1)
                    nodes(redo, True)

            @block.vector
            def _(dve):
                steps = [0]

                def link(ins):
                    steps[0] += 1
                    ins.then_inc(s_dc, 1)
                    dve.wait_ge(s_dc, steps[0])

                for t in (wfc1, wsk_a, wsk_z, wnl_a, wnl_z, msg, tp_s, row0, zeros_w):
                    last = dve.memset(t[:], 0.0)
                link(last)
                link(dve.memset(row0[:, LOCAL:LOCAL + 1], -1.0))
                dve.memset(zeros_bf[:], 0.0).then_inc(s_clr, 1)
                dve.wait_ge(s_in, 48)
                dve.wait_ge(s_const, 7)
                link(dve.tensor_tensor(vec_sq[:], vec[:], vec[:], ALU.mult))
                link(dve.tensor_tensor(vec_d2[:], vec_sq[:, :, 0], vec_sq[:, :, 1], ALU.add))
                dve.tensor_tensor(vec_d2[:], vec_d2[:], vec_sq[:, :, 2], ALU.add).then_inc(s_tab, 1)
                dve.tensor_copy(iota_bin[:], iota_i[:, 0:NB])
                dve.tensor_copy(iota_slot[:], iota_i[:, 0:CAP])
                dve.tensor_copy(iota_local[:], iota_i[:, 0:2 * P])
                link(dve.tensor_scalar(tmp_a[:], src_i[:], 10, 2, ALU.logical_shift_right, ALU.logical_shift_left))
                link(dve.tensor_scalar(tmp_b[:], src_i[:], 1, BPM - 1, ALU.logical_shift_right, ALU.bitwise_and))
                link(dve.tensor_tensor(bin_of[:], tmp_a[:], tmp_b[:], ALU.add))
                link(dve.tensor_scalar(tmp_a[:], src_i[:], 3, P - 1, ALU.logical_shift_right, ALU.bitwise_and))
                link(dve.tensor_scalar(tmp_b[:], src_i[:], 1, 7, ALU.bitwise_and, ALU.logical_shift_left))
                link(dve.tensor_tensor(place_of[:, :, 0], tmp_a[:], tmp_b[:], ALU.add))
                dve.tensor_copy(place_of[:, :, 1], src_i[:])
                link(dve.tensor_scalar(tmp_a[:], num_i[:], 7, None, ALU.logical_shift_right))
                link(dve.tensor_scalar(tmp_b[:], num_i[:], P - 1, None, ALU.bitwise_and))
                link(dve.tensor_copy(num_hi[:], tmp_a[:]))
                link(dve.tensor_copy(num_lo[:], tmp_b[:]))
                dve.wait_ge(s_r, 1)
                link(dve.tensor_tensor(hat[:, :, 0:3], vec[:], vec_r[:, :].unsqueeze(2).to_broadcast((ET, NT, 3)), ALU.mult))
                dve.tensor_copy(hat[:, :, 3], hat[:, :, 0]).then_inc(s_tab, 1)
                dve.wait_ge(s_tab, 2)
                dve.wait_ge(s_w, 16 * 18)
                dve.tensor_scalar(wos[:], wos[:], 1.0 / 32.0, None, ALU.mult)
                dve.tensor_scalar(wov[0:64, :], wov[0:64, :], 3.0 ** 0.5 / 32.0, None, ALU.mult)
                dve.tensor_scalar(wov[64:96, :], wov[64:96, :], 1.0 / 32.0, None, ALU.mult)
                link(dve.tensor_scalar(wov[96:128, :], wov[96:128, :], 1.5 ** 0.5 / 32.0, None, ALU.mult))
                dve.memset(most[:], 0.0).then_inc(s_wready, 1)

                def round_b(q):
                    for k in range(GE):
                        t = q * GE + k
                        wait(dve, b_tab, t - GE + 1)
                        dve.tensor_scalar(bin_hot[:, k, :], iota_bin[0:ET, :], bin_of[:, bass.ds(t, 1)], None,
                                          ALU.is_equal).then_inc(b_hot, 1)
                    for k in range(GE):
                        t = q * GE + k
                        dve.wait_ge(b_pre, t + 1)
                        dve.tensor_tensor_reduce(out=rank_junk[:], in0=bin_hot[:, k, :], in1=p_cnt, scale=1.0,
                                                 scalar=0.0, op0=ALU.mult, op1=ALU.add,
                                                 accum_out=rank[:, k:k + 1]).then_inc(b_rank, 1)
                        dve.wait_ge(b_rank, t + 1)
                        dve.tensor_scalar(slot_hi[:, k, :], iota_slot[0:ET, :], rank[:, k:k + 1],
                                          num_hi[:, bass.ds(t, 1)], ALU.is_equal, ALU.mult)
                        dve.tensor_scalar(slot_lo[:, k, :], iota_slot[0:ET, :], rank[:, k:k + 1],
                                          num_lo[:, bass.ds(t, 1)], ALU.is_equal, ALU.mult).then_inc(b_slot, 1)

                round_b(0)
                with dve.Fori(1, NG) as q:
                    round_b(q)
                dve.wait_ge(b_end, 1)
                dve.reduce_max(most[:], p_cnt, AX_X).then_inc(b_most, 1)
                dve.wait_ge(b_most, 1)
                dve.tensor_copy(most_i[:], most[:])
                dve.wait_ge(b_lo, 1)
                dve.scalar_tensor_tensor(out=slots_i[:], in0=p_hi, scalar=float(P), in1=tab_lo[:],
                                         op0=ALU.mult, op1=ALU.add).then_inc(b_fin, 1)

                def layer_norm(rows, stat, sums, chain, base, done):
                    for t in range(rows.shape[1]):
                        last = dve.bn_stats(stat[:, t, :], rows[:, t, :])
                    last.then_inc(chain, 1)
                    dve.wait_ge(chain, base + 1)
                    dve.tensor_tensor(sums[:, 0, :], stat[:, :, 1], stat[:, :, 4], ALU.subtract)
                    dve.tensor_tensor(sums[:, 1, :], stat[:, :, 2], stat[:, :, 5], ALU.add)
                    dve.tensor_tensor(sums[:, 2, :], stat[:, :, 1], stat[:, :, 4], ALU.add).then_inc(chain, 1)
                    dve.wait_ge(chain, base + 2)
                    dve.tensor_tensor(sums[:, 3, :], sums[:, 0, :], sums[:, 0, :], ALU.mult)
                    dve.tensor_scalar(sums[:, 1, :], sums[:, 1, :], 1.0 / F, EPS, ALU.mult, ALU.add)
                    dve.tensor_scalar(sums[:, 2, :], sums[:, 2, :], -0.5, None, ALU.mult).then_inc(chain, 1)
                    dve.wait_ge(chain, base + 3)
                    dve.scalar_tensor_tensor(out=sums[:, 4, :], in0=sums[:, 3, :], scalar=0.25,
                                             in1=sums[:, 1, :], op0=ALU.mult, op1=ALU.add).then_inc(done, 1)

                def round_e(q, b, front, back):
                    if front:
                        dve.wait_ge(e_x[b], 64 * (q // 2) + 64 if isinstance(q, int) else 32 * q + (64 if b == 0 else 32))
                        wait(dve, e_ln, q - 1)
                        layer_norm(xg[:, b, :, :], e_stat[:, b, :, :], e_sum[:, b, :, :], e_c, 3 * q, e_var)
                    if back:
                        p, c = q - 1, 1 - b
                        w = w_sb[:, c, :, :]
                        h3 = hat[:, bass.ds(p * GE, GE), 0:3].unsqueeze(3).to_broadcast((ET, GE, 3, V))
                        h = hat[:, bass.ds(p * GE, GE), :]
                        dve.wait_ge(e_wsb, p + 1)
                        dve.wait_ge(e_xs, p + 1)
                        wait(dve, e_gp, p)
                        wait(dve, e_tt, GE * p)
                        dve.tensor_tensor(w1xs[:], w[:, :, S:2 * S], p_xs, ALU.mult)
                        dve.tensor_tensor(w4xv[:], w[:, :, W - V:W].unsqueeze(2).to_broadcast((ET, GE, 3, V)),
                                          p_xv, ALU.mult).then_inc(e_t1, 1)
                        dve.tensor_tensor(xvh[:], h3, p_xv, ALU.mult).then_inc(e_c2, 1)
                        dve.tensor_tensor(tp_s[:, :, 0:S], w[:, :, 0:S], p_xs, ALU.mult)
                        dve.tensor_tensor(tp_v[:, :, :, S:S + V],
                                          w[:, :, 2 * S:2 * S + V].unsqueeze(2).to_broadcast((ET, GE, 3, V)),
                                          p_xv, ALU.mult).then_inc(e_px, 1)
                        dve.wait_ge(e_c2, 3 * p + 1)
                        dve.tensor_tensor(dot[:, 0, :, :], xvh[:, :, 0, :], xvh[:, :, 1, :], ALU.add).then_inc(e_c2, 1)
                        dve.wait_ge(e_t1, p + 1)
                        dve.tensor_tensor(cr_b[:, :, 0, :], w4xv[:, :, 2, :], h[:, :, 1:2].to_broadcast((ET, GE, V)), ALU.mult)
                        dve.wait_ge(e_c2, 3 * p + 2)
                        dve.tensor_tensor(dot[:, 1, :, :], dot[:, 0, :, :], xvh[:, :, 2, :], ALU.add).then_inc(e_c2, 1)
                        dve.tensor_tensor(cr_b[:, :, 1:3, :], w4xv[:, :, 0:2, :],
                                          h[:, :, 2:4].unsqueeze(3).to_broadcast((ET, GE, 2, V)), ALU.mult).then_inc(e_c3, 1)
                        dve.wait_ge(e_c2, 3 * p + 3)
                        dve.tensor_tensor(tp_s[:, :, S:SG], dot[:, 1, :, :], w[:, :, 2 * S + V:2 * S + 2 * V], ALU.mult)
                        dve.wait_ge(e_c3, p + 1)
                        dve.wait_ge(e_gp, p + 1)
                        dve.tensor_tensor(tp_v[:, :, :, S + V:P], cr_a[:], cr_b[:], ALU.subtract).then_inc(e_tp, 1)
                        if isinstance(p, int):
                            wait(dve, e_st[c], 16 * (p // 2))
                        else:
                            dve.wait_ge(e_st[c], 8 * p - (8 if c == 1 else 0))
                        dve.tensor_copy(msg[:, c, :, LOCAL:NODE + 1], place_of[:, bass.ds(p * GE, GE), :]).then_inc(e_loc, 1)

                groups(dve, round_e)

                def nodes(n, every):
                    def stats_n(i, u):
                        loads = i // U if isinstance(i, int) else (i - u) // U
                        dve.wait_ge(n.x[u], 16 * loads + 16)
                        wait(dve, n.norm, 2 * (i - U) + 2)
                        layer_norm(xb[:, u, :, :], n_stat[:, u, :, :], n_sum[:, u, :, :], n.c, 3 * i, n.var)

                    def hot_n(i, u):
                        loads = i // U if isinstance(i, int) else (i - u) // U
                        dve.wait_ge(n.g[u], 64 * loads + 64)
                        wait(dve, n.z, 2 * (i - U) + 2)
                        for k in range(BPM):
                            last = dve.tensor_scalar(hot[:, u, k, :], iota_local[:], mg[:, u, k, LOCAL:LOCAL + 1],
                                                     None, ALU.is_equal)
                        last.then_inc(n.hot, 1)

                    def places(i):
                        def chunk(k, b):
                            c = i * NC + k
                            dve.wait_ge(r_m[b], (c + (2 if b == 0 else 1)) // 2 * 16 if isinstance(c, int)
                                        else (c + (2 if b == 0 else 1)) * 8)
                            dve.tensor_scalar(rel[:, b, :], again[:, b, :, NODE], macro_base[:, :], None,
                                              ALU.subtract).then_inc(r_rel, 1)
                            dve.wait_ge(r_rel, c + 1)
                            for t in range(RC):
                                m = c * RC + t
                                dve.wait_ge(r_used, m - 1 + CREDIT)
                                dve.tensor_scalar(key_hot[:, t % 2, :], iota_key[:], rel[:, b, t:t + 1], None,
                                                  ALU.is_equal).then_inc(n.hot, 1)

                        chunks(dve, chunk)
                        dve.tensor_scalar(macro_base[:], macro_base[:], float(MN), None, ALU.add).then_inc(r_base, 1)
                        dve.wait_ge(r_base, i + 1)

                    stats_n(0, 0)
                    if not every:
                        hot_n(0, 0)

                    def round_n(i, u):
                        if not (isinstance(i, int) and i + 1 >= NM):
                            stats_n(i + 1, (u + 1) % U)
                            if not every:
                                hot_n(i + 1, (u + 1) % U)
                        if every:
                            places(i)
                        if isinstance(i, int):
                            wait(dve, n.st[u], 16 * (i // U))
                        else:
                            dve.wait_ge(n.st[u], (i - u) // U * 16)
                        for h in range(2):
                            dve.wait_ge(n.sg, 2 * i + h + 1)
                            z = q_z[h]
                            o = ob[:, u, 4 * h:4 * h + 4, :]
                            dve.tensor_tensor(o[:, :, 0:S], z[:, :, 0:S], sg[:, h, :, 0:S], ALU.mult)
                            dve.tensor_tensor(o[:, :, S:F].rearrange("p t (i k) -> p t i k", i=3),
                                              z[:, :, SG:Z].rearrange("p t (i k) -> p t i k", i=3),
                                              sg[:, h, :, S:SG].unsqueeze(2).to_broadcast((P, 4, 3, V)),
                                              ALU.mult).then_inc(n.mul, 1)

                    macros(dve, round_n)

                nodes(main, False)
                dve.wait_ge(b_fin, 1)
                with dve.If(dve.value_load(most_i[0:1, 0:1]) > CAP):
                    dve.wait_ge(r_iota, 1)
                    for g in range(2):
                        dve.tensor_scalar(iota_key[:, 512 * g:512 * g + 512], iota_i[0:ET, :], float(4 * g), None, ALU.add)
                    dve.memset(macro_base[:], 0.0).then_inc(r_key, 1)
                    dve.wait_ge(r_key, 1)
                    nodes(redo, True)

            @block.scalar
            def _(act):
                act.wait_ge(b_end, 1)
                act.activation(tab_lo[:], p_lo, ACT.Copy).then_inc(b_lo, 1)

                def round_e(q, b, front, back):
                    if front:
                        act.wait_ge(e_ln, q + 1)
                        wait(act, e_t, q - 1)
                        for t in range(GE):
                            last = act.activation(hn[:, b, :, t], xg[:, b, t, :], ACT.Relu,
                                                  bias=e_bias[:, b, t:t + 1], scale=e_rstd[:, b, t:t + 1])
                        last.then_inc(e_norm, 1)
                        act.wait_ge(e_t, q + 1)
                        wait(act, e_xs, q)
                        act.activation(ht[:], p_t, ACT.Copy)
                        act.activation(hz[:], p_tz, ACT.Copy).then_inc(e_ht, 1)
                        act.wait_ge(e_h1, q + 1)
                        wait(act, e_w, q)
                        act.activation(hid[:], p_h[0:EF, :], ACT.Relu).then_inc(e_hid, 1)
                        act.wait_ge(e_w, q + 1)
                        wait(act, e_tp, q - 1)
                        act.activation(w_sb[:, b, :, :], p_w, ACT.Copy).then_inc(e_wsb, 1)
                    if back:
                        p, c = q - 1, 1 - b

                        def take(t):
                            act.wait_ge(e_tt, GE * p + t + 1)
                            wait(act, e_m, GE * p + t - 1)
                            act.activation(tpt[:, t % 2, :], p_tt, ACT.Copy).then_inc(e_ttsb, 1)

                        def put(j):
                            act.wait_ge(e_m, GE * p + 2 * j + 2)
                            if j == 0:
                                if isinstance(p, int):
                                    wait(act, e_st[c], 16 * (p // 2))
                                else:
                                    act.wait_ge(e_st[c], 8 * p - (8 if c == 1 else 0))
                            act.activation(msg[:, c, 2 * j:2 * j + 2, 0:Z], p_m, ACT.Copy).then_inc(e_msb, 1)

                        take(0)
                        take(1)
                        put(0)
                        take(2)
                        take(3)
                        put(1)

                groups(act, round_e)

                def nodes(n, every):
                    def norm(i, u, h):
                        act.wait_ge(n.ln, i + 1)
                        wait(act, n.t, 2 * (i - U) + 2)
                        for g in range(4 * h, 4 * h + 4):
                            last = act.activation(nn[:, u, h, :, g % 4], xb[:, u, g, :], ACT.Relu,
                                                  bias=n_bias[:, u, g:g + 1], scale=n_rstd[:, u, g:g + 1])
                        last.then_inc(n.norm, 1)

                    norm(0, 0, 0)
                    norm(0, 0, 1)

                    def round_n(i, u):
                        for h in range(2):
                            act.wait_ge(n.t, 2 * i + h + 1)
                            wait(act, n.z, 2 * i + h - 1)
                            act.activation(nt_a[:, h, :], q_t[h], ACT.Copy)
                            act.activation(nt_z[:, h, :], q_tz[h], ACT.Copy).then_inc(n.ht, 1)
                        if not (isinstance(i, int) and i + 1 >= NM):
                            norm(i + 1, (u + 1) % U, 0)
                            norm(i + 1, (u + 1) % U, 1)
                        for h in range(2):
                            act.wait_ge(n.z, 2 * i + h + 1)
                            wait(act, n.mul, 2 * i + h - 1)
                            act.activation(sg[:, h, :, :], q_z[h][:, :, 0:SG], ACT.Sigmoid).then_inc(n.sg, 1)

                    macros(act, round_n)

                nodes(main, False)
                act.wait_ge(b_fin, 1)
                with act.If(act.value_load(most_i[0:1, 0:1]) > CAP):
                    nodes(redo, True)

            @block.tensor
            def _(pe):
                pe.wait_ge(s_wready, 1)
                for o in (p_cnt, p_hi, p_lo):
                    pe.matmul(o, zeros_bf[0:ET, 0:o.shape[0]], zeros_bf[0:ET, :], start=True, stop=False,
                              skip_group_check=True)

                def round_b(q):
                    for k in range(GE):
                        t = q * GE + k
                        if k == 0:
                            pe.wait_ge(b_hot, t + 1)
                            pe.matmul(p_cnt, tri_before[:], bin_hot[:, 0, :], start=False, stop=False,
                                      skip_group_check=True).then_inc(b_pre, 1)
                        pe.wait_ge(b_rank, t + 1)
                        pe.matmul(p_cnt, tri_rest[:], bin_hot[:, k, :], start=False, stop=False,
                                  skip_group_check=True)
                        if k + 1 < GE:
                            pe.wait_ge(b_hot, t + 2)
                            pe.matmul(p_cnt, tri_before[:], bin_hot[:, k + 1, :], start=False, stop=False,
                                      skip_group_check=True).then_inc(b_pre, 1)
                        pe.wait_ge(b_slot, t + 1)
                        pe.matmul(p_hi, slot_hi[:, k, :], bin_hot[:, k, :], start=False, stop=False,
                                  skip_group_check=True)
                        pe.matmul(p_lo, slot_lo[:, k, :], bin_hot[:, k, :], start=False, stop=False,
                                  skip_group_check=True).then_inc(b_tab, 1)

                with pe.Fori(0, NG) as q:
                    round_b(q)
                for o in (p_cnt, p_hi, p_lo):
                    last = pe.matmul(o, zeros_bf[0:ET, 0:o.shape[0]], zeros_bf[0:ET, :], start=False, stop=True,
                                     skip_group_check=True)
                last.then_inc(b_end, 1)
                pe.wait_ge(b_fin, 1)

                idt = ident[0:ET, 0:ET]

                def round_e(q, b, front, back):
                    if front:
                        pe.wait_ge(e_norm, q + 1)
                        wait(pe, e_ht, q)
                        for t in range(GE):
                            pe.transpose(p_t[:, t * ET:(t + 1) * ET], hn[:, b, 0:P, t], idt)
                        pe.transpose(p_tz, hn[:, b, P:F, :], idt).then_inc(e_t, 1)
                        if isinstance(q, int):
                            pe.wait_ge(e_f[b], 16 * (q // 2) + 16)
                        else:
                            pe.wait_ge(e_f[b], 8 * q + (8 if b == 1 else 16))
                        wait(pe, e_msb, 2 * q - 2)
                        pe.matmul(p_h, wfc1[:], ef[:, b, :], start=True, stop=True).then_inc(e_h1, 1)
                        pe.wait_ge(e_hid, q + 1)
                        wait(pe, e_wsb, q)
                        for t in range(GE):
                            last = pe.matmul(p_w[:, t, :], hid[:, t * ET:(t + 1) * ET], wfc2[:], start=True, stop=True)
                        last.then_inc(e_w, 1)
                        pe.wait_ge(e_ht, q + 1)
                        wait(pe, e_px, q)
                        for t in range(GE):
                            pe.matmul(p_x[:, t, 0:P], ht[:, t * ET:(t + 1) * ET], wnl_a[:],
                                      start=(t % 2 == 0), stop=True, skip_group_check=True)
                        for j in range(2):
                            last = pe.matmul(p_x[:, 2 * j:2 * j + 2, P:F], hz[:], wnl_z[:, 2 * V * j:2 * V * j + 2 * V],
                                             start=False, stop=True, skip_group_check=True)
                        last.then_inc(e_xs, 1)
                    if back:
                        p = q - 1
                        pe.wait_ge(e_tp, p + 1)

                        def turn(t):
                            pe.transpose(p_tt[:, 0:ET], tp_s[:, t, :], idt)
                            for i in range(3):
                                last = pe.transpose(p_tt[:, (i + 1) * ET:(i + 2) * ET], tp_v[:, t, i, :], idt)
                            last.then_inc(e_tt, 1)

                        wait(pe, e_ttsb, GE * p)
                        turn(0)
                        for t in range(GE):
                            pe.wait_ge(e_ttsb, GE * p + t + 1)
                            if t + 1 < GE:
                                turn(t + 1)
                            if t == 2:
                                pe.wait_ge(e_msb, 2 * p + 1)
                            elif t == 0 and not front:
                                pe.wait_ge(e_msb, 2 * p)
                            elif t == 0:
                                pe.wait_ge(e_hid, q + 1)
                            a = tpt[:, t % 2, :]
                            pe.matmul(p_m[:, t % 2, 0:SG], a[0:SG, 0:ET], wos[:], start=(t % 2 == 0), stop=True,
                                      skip_group_check=True)
                            for i in range(3):
                                last = pe.matmul(p_m[:, t % 2, SG + V * i:SG + V * i + V],
                                                 a[:, (i + 1) * ET:(i + 2) * ET], wov[:], start=False, stop=True,
                                                 skip_group_check=True)
                            last.then_inc(e_m, 1)

                groups(pe, round_e)
                pe.wait_ge(e_msb, 2 * NG)

                def nodes(n, every):
                    def turn(i, u, h):
                        pe.wait_ge(n.norm, 2 * i + h + 1)
                        wait(pe, n.ht, 2 * i + h - 1)
                        for t in range(4):
                            pe.transpose(q_t[h][:, t * P:(t + 1) * P], nn[:, u, h, 0:P, t], ident[:])
                        pe.transpose(q_tz[h], nn[:, u, h, P:F, :], ident[:]).then_inc(n.t, 1)

                    def skip(i, h):
                        z = q_z[h]
                        pe.wait_ge(n.ht, 2 * i + h + 1)
                        wait(pe, n.mul, 2 * i + h - 1)
                        for t in range(4):
                            pe.matmul(z[:, t, 0:F], nt_a[:, h, t * P:(t + 1) * P], wsk_a[:], start=(t % 2 == 0),
                                      stop=False, skip_group_check=True)
                        for j in range(2):
                            last = pe.matmul(z[:, 2 * j:2 * j + 2, F:Z], nt_z[:, h, :],
                                             wsk_z[:, 2 * V * j:2 * V * j + 2 * V],
                                             start=False, stop=every, skip_group_check=True)
                        return last

                    def add(i, u, h):
                        if h == 0:
                            pe.wait_ge(n.hot, i + 1)
                        for t in range(4):
                            g = 4 * h + t
                            last = pe.matmul(q_z[h][:, t, 0:Z], hot[:, u, g // 2, (g % 2) * P:(g % 2) * P + P],
                                             mg[:, u, g // 2, 0:Z], start=False, stop=True, skip_group_check=True)
                        last.then_inc(n.z, 1)

                    def add_every(i):
                        def chunk(k, b):
                            for t in range(RC):
                                pe.wait_ge(n.hot, (i * NC + k) * RC + t + 1)
                                for g in range(G):
                                    last = pe.matmul(q_z[g // 4][:, g % 4, 0:Z], key_hot[:, t % 2, g * P:g * P + P],
                                                     again[:, b, t, 0:Z], start=False, stop=True, skip_group_check=True)
                                last.then_inc(r_used, 1)

                        chunks(pe, chunk)
                        for h in range(2):
                            pe.matmul(q_z[h][:, 0, 0:Z], zeros_w[:], again[:, 0, 0, 0:Z], start=False, stop=True,
                                      skip_group_check=True).then_inc(n.z, 1)

                    def round_n(i, u):
                        turn(i, u, 0)
                        turn(i, u, 1)
                        for h in range(2):
                            skip(i, h)
                            if not every:
                                add(i, u, h)
                        if every:
                            add_every(i)

                    macros(pe, round_n)

                nodes(main, False)
                pe.wait_ge(b_fin, 1)
                with pe.If(pe.value_load(most_i[0:1, 0:1]) > CAP):
                    pe.sem_inc(r_used, CREDIT)
                    nodes(redo, True)


_WEIGHTS = ["W_skip0", "W_skip1", "W_nl0", "W_nl1", "W_fc1", "W_fc2", "W_out_s", "W_out_v"]


def _swap(a, rows, cols):
    import numpy as _np
    n = a.shape[0]
    v = a[:, 64:].reshape(n, rows, cols).transpose(0, 2, 1).reshape(n, rows * cols)
    return _np.ascontiguousarray(_np.concatenate([a[:, :64], v], axis=1))


def layout(inputs):
    import numpy as _np
    et = 125
    arrays = {"x": _swap(_np.asarray(inputs["x"]), 32, 3)}
    for name in ("src", "dst"):
        a = _np.asarray(inputs[name])
        arrays[name] = _np.ascontiguousarray(a.reshape(-1, et).T)
    v = _np.asarray(inputs["edge_attr_3"])
    arrays["edge_vec"] = _np.ascontiguousarray(v.reshape(-1, et, 3).transpose(1, 0, 2))
    arrays["edge_feat_t"] = _np.ascontiguousarray(_np.asarray(inputs["edge_attr_64"]).T)
    for name in _WEIGHTS:
        arrays[name] = _np.ascontiguousarray(_np.asarray(inputs[f"L0_gnn_{name}"]))
    return arrays


def kernel(**inputs):
    import concourse.bacc as _bacc
    from concourse import mybir as _mybir
    from concourse.bass_utils import run_bass_kernel_spmd as _run

    arrays = layout(inputs)
    nc = _bacc.Bacc("TRN2", target_bir_lowering=False, num_devices=1)
    args = [nc.dram_tensor(n, a.shape, _mybir.dt.from_np(a.dtype), kind="ExternalInput").ap()
            for n, a in arrays.items()]
    out = nc.dram_tensor("out_0_dram", arrays["x"].shape, _mybir.dt.float32, kind="ExternalOutput").ap()
    gnn_layer(nc, *args, out)
    r = _run(nc, [arrays], core_ids=[0])
    return _swap(r.results[0]["out_0_dram"], 3, 32)
```

```python
from contextlib import ExitStack

import concourse.bass as bass
from concourse import mybir

ALU = mybir.AluOpType
ACT = mybir.ActivationFunctionType
F32 = mybir.dt.float32
F16 = mybir.dt.float16
BF16 = mybir.dt.bfloat16
I32 = mybir.dt.int32
AX_X = mybir.AxisListType.X

P = 128
EPS = 1e-5


def gnn_layer(nc, x, src, dst, edge_vec, edge_feat_t, w_skip0, w_skip1, w_nl0, w_nl1,
              w_fc1, w_fc2, w_out_s, w_out_v, out):
    N, F = x.shape
    S = w_skip0.shape[0]
    V = w_skip1.shape[0]
    SG = w_skip0.shape[1]
    W = w_fc2.shape[1]
    Z = SG + 3 * V
    assert (S, V, F, SG, W) == (64, 32, 160, 96, 224)

    ET, NT = src.shape
    GE = 4
    NG = NT // GE
    EF = edge_feat_t.shape[0]
    assert NT % GE == 0 and NT % 8 == 0

    G = 8
    MN = P * G
    NM = -(-N // MN)
    LAST_P = (N - (NM - 1) * MN) // G
    assert N % G == 0
    BPM = G // 2
    NB = NM * BPM
    CAP = P
    MW = 200
    LOCAL, NODE = Z, Z + 1
    CORE = GE * 64
    TS = 256

    messages = nc.dram_tensor("messages", (1 + ET * NT, MW), F32).ap()

    with ExitStack() as ctx:
        def sb(name, shape, dt=F32):
            return ctx.enter_context(nc.sbuf_tensor(name, shape, dt))

        def sem(name):
            return ctx.enter_context(nc.semaphore(name))

        ident = sb("ident", [P, P])
        tri_before = sb("tri_before", [ET, ET], BF16)
        tri_rest = sb("tri_rest", [ET, ET], BF16)
        ones_bf = sb("ones_bf", [ET, ET], BF16)
        iota_i = sb("iota_i", [P, 512], I32)
        iota_bin = sb("iota_bin", [P, NB], F16)
        iota_slot = sb("iota_slot", [P, CAP], F16)
        iota_local = sb("iota_local", [P, 2 * P])
        zeros_bf = sb("zeros_bf", [P, NB], BF16)
        neg_half = sb("neg_half", [P, G])
        src_i = sb("src_i", [ET, NT], I32)
        dst_i = sb("dst_i", [ET, NT], I32)
        num_i = sb("num_i", [ET, NT], I32)
        tmp_a = sb("tmp_a", [ET, NT], I32)
        tmp_b = sb("tmp_b", [ET, NT], I32)
        bin_of = sb("bin_of", [ET, NT])
        place_of = sb("place_of", [ET, NT, 2])
        num_hi = sb("num_hi", [ET, NT])
        num_lo = sb("num_lo", [ET, NT])
        neg_hi = sb("neg_hi", [ET, NT])
        neg_lo = sb("neg_lo", [ET, NT])
        vec = sb("vec", [ET, NT, 3])
        vec_sq = sb("vec_sq", [ET, NT, 3])
        vec_d2 = sb("vec_d2", [ET, NT])
        vec_r = sb("vec_r", [ET, NT])
        half_nt = sb("half_nt", [ET, NT])
        hat = sb("hat", [ET, NT, 4])
        slots_i = sb("slots_i", [CAP, NB], I32)
        tab_lo = sb("tab_lo", [CAP, NB])
        most = sb("most", [ET, 1])
        most_i = sb("most_i", [ET, 1], I32)

        wsk_a = sb("wsk_a", [P, SG + 2 * V])
        wsk_z = sb("wsk_z", [P, 4 * V])
        wnl_a = sb("wnl_a", [P, S + 2 * V])
        wnl_z = sb("wnl_z", [P, 4 * V])
        wfc1 = sb("wfc1", [EF, P])
        wfc2 = sb("wfc2", [EF, W])
        wos = sb("wos", [SG, SG])
        wov = sb("wov", [P, V])

        BR = 8
        bin_hot = sb("bin_hot", [ET, BR, NB], BF16)
        rank_junk = sb("rank_junk", [ET, 2, NB], BF16)
        rank = sb("rank", [ET, BR])
        off_slot = sb("off_slot", [ET, GE, CAP])
        slot_hi = sb("slot_hi", [ET, GE, CAP], BF16)
        slot_lo = sb("slot_lo", [ET, GE, CAP], BF16)

        D = 4
        msg = sb("msg", [ET, 2, GE, MW])
        zeros_w = sb("zeros_w", [ET, P])
        row0 = sb("row0", [1, MW])

        with ExitStack() as msg_ctx:
            def sb_msg(name, shape, dt=F32):
                return msg_ctx.enter_context(nc.sbuf_tensor(name, shape, dt))

            dst_g = sb_msg("dst_g", [ET, D, GE], I32)
            xg = sb_msg("xg", [ET, D, GE, F])
            ef = sb_msg("ef", [EF, 2, GE * ET])
            e_stat = sb_msg("e_stat", [ET, D, GE, 6])
            e_sum = sb_msg("e_sum", [ET, D, 5, GE])
            e_rstd = sb_msg("e_rstd", [ET, D, GE])
            e_bias = sb_msg("e_bias", [ET, D, GE])
            hn = sb_msg("hn", [ET, 2, F, GE])
            ht = sb_msg("ht", [P, 2, GE * ET])
            hz = sb_msg("hz", [P, 2, ET])
            hid = sb_msg("hid", [EF, GE * ET])
            w_sb = sb_msg("w_sb", [ET, 2, GE, W])
            tp_s = sb_msg("tp_s", [ET, 2, GE, P])
            tp_v = sb_msg("tp_v", [ET, 2, GE, 3, P])
            w1xs = sb_msg("w1xs", [ET, GE, S])
            xvh = sb_msg("xvh", [ET, GE, 3, V])
            dot = sb_msg("dot", [ET, 2, GE, V])
            w4xv = sb_msg("w4xv", [ET, GE, 3, V])
            cr_a = sb_msg("cr_a", [ET, GE, 3, V])
            cr_b = sb_msg("cr_b", [ET, GE, 3, V])
            tpt = sb_msg("tpt", [P, 2, 4 * ET])

        RC = 10
        NC = NT // RC
        CREDIT = 2 * RC
        again = sb("again", [ET, 2, RC, MW])
        rel = sb("rel", [ET, 2, RC])
        macro_base = sb("macro_base", [ET, 1])
        iota_key = sb("iota_key", [ET, MN])
        key_hot = sb("key_hot", [ET, 2, MN])

        U = 4
        RP = 2
        xb = sb("xb", [P, U, G, F])
        n_stat = sb("n_stat", [P, U, G, 6])
        n_sum = sb("n_sum", [P, U, 5, G])
        n_rstd = sb("n_rstd", [P, U, G])
        n_bias = sb("n_bias", [P, U, G])
        nn = sb("nn", [P, 2, 2, F, 4])
        slot_m = sb("slot_m", [P, U, BPM], I32)
        mg = sb("mg", [P, U, BPM, MW])
        hot = sb("hot", [P, 2, BPM, 2 * P])
        nt_a = sb("nt_a", [P, 2, 4 * P])
        nt_z = sb("nt_z", [P, 2, P])
        sg = sb("sg", [P, 2, 4, SG])
        ob = sb("ob", [P, U, G, F])

        s_in = sem("s_in")
        s_w = sem("s_w")
        s_clr = sem("s_clr")
        s_const = sem("s_const")
        s_pc = sem("s_pc")
        s_dc = sem("s_dc")
        s_tab = sem("s_tab")
        s_r = sem("s_r")
        s_wready = sem("s_wready")
        s_row0 = sem("s_row0")
        s_held = sem("s_held")

        b_hot = sem("b_hot")
        b_pre = sem("b_pre")
        b_rank = sem("b_rank")
        b_off = sem("b_off")
        b_slot = sem("b_slot")
        b_const = sem("b_const")
        b_tab = sem("b_tab")
        b_lo = sem("b_lo")
        b_most = sem("b_most")
        b_end = sem("b_end")
        b_fin = sem("b_fin")

        e_idx = sem("e_idx")
        e_x = [sem(f"e_x{b}") for b in range(D)]
        e_f = [sem("e_f0"), sem("e_f1")]
        e_c2 = sem("e_c2")
        e_c3 = sem("e_c3")
        e_c4 = sem("e_c4")
        e_c = sem("e_c")
        e_var = sem("e_var")
        e_pw = sem("e_pw")
        e_ln = sem("e_ln")
        e_norm = sem("e_norm")
        e_t = sem("e_t")
        e_ht = sem("e_ht")
        e_h1 = sem("e_h1")
        e_hid = sem("e_hid")
        e_w = sem("e_w")
        e_wsb = sem("e_wsb")
        e_xs = sem("e_xs")
        e_px = sem("e_px")
        e_t1 = sem("e_t1")
        e_gp = sem("e_gp")
        e_tp = sem("e_tp")
        e_tt = sem("e_tt")
        e_ttsb = sem("e_ttsb")
        e_m = sem("e_m")
        e_msb = sem("e_msb")
        e_st = [sem("e_st0"), sem("e_st1")]

        class Nodes:

            def __init__(self, name):
                self.x = [sem(f"{name}_x{u}") for u in range(U)]
                self.idx = sem(f"{name}_idx")
                self.g = [sem(f"{name}_g{u}") for u in range(U)]
                self.c = sem(f"{name}_c")
                self.var = sem(f"{name}_var")
                self.pw = sem(f"{name}_pw")
                self.ln = sem(f"{name}_ln")
                self.norm = sem(f"{name}_norm")
                self.t = sem(f"{name}_t")
                self.ht = sem(f"{name}_ht")
                self.hot = sem(f"{name}_hot")
                self.z = sem(f"{name}_z")
                self.sg = sem(f"{name}_sg")
                self.mul = sem(f"{name}_mul")
                self.res = [sem(f"{name}_res{h}") for h in range(2)]
                self.st = [sem(f"{name}_st{u}") for u in range(U)]

        main = Nodes("n")
        redo = Nodes("r")
        r_iota = sem("r_iota")
        r_key = sem("r_key")
        r_m = [sem("r_m0"), sem("r_m1")]
        r_rel = sem("r_rel")
        r_base = sem("r_base")
        r_used = sem("r_used")

        def wait(eng, s, value):
            if not (isinstance(value, int) and value <= 0):
                eng.wait_ge(s, value)

        def earlier(q, b, depth, per):
            return q // depth * per if isinstance(q, int) else (q - b) * (per // depth)

        def edge_tiles(eng, body):
            def round_b(q):
                for k in range(BR):
                    body(q * BR + k, k)

            round_b(0)
            with eng.Fori(1, NT // BR - 1) as q:
                round_b(q)
            round_b(NT // BR - 1)

        def tile_exists(t):
            return not isinstance(t, int) or 0 <= t < NT

        def groups(eng, body):
            loops = (NG - 3 - D) // D
            for q in range(D):
                body(q, q % D)
            with eng.Fori(0, loops) as r:
                for b in range(D):
                    body(D * r + (D + b), b)
            for q in range(D * (loops + 1), NG + 3):
                body(q, q % D)

        def within(q):
            return not isinstance(q, int) or 0 <= q < NG

        def chunks(eng, body):
            with eng.Fori(0, NC // 2) as r:
                body(2 * r, 0)
                body(2 * r + 1, 1)

        def macros(eng, body):
            full = (NM - 4 - U) // U
            for i in range(U):
                body(i, i % U)
            with eng.Fori(0, full) as r:
                for u in range(U):
                    body(U * r + (U + u), u)
            for i in range(U + U * full, NM):
                body(i, i % U)

        def macro_exists(i):
            return not isinstance(i, int) or 0 <= i < NM

        with ExitStack() as psum_ctx:
            def ps(name, shape, dt=F32):
                return psum_ctx.enter_context(nc.psum_tensor(name, shape, dt))

            bank = [ps(f"bank{i}", [P, 1024]) for i in range(4)]

            p_cnt = [bank[0][0:ET, 512 * j:512 * j + NB] for j in range(2)]
            p_hi = bank[1][:, 0:NB]
            p_lo = bank[2][:, 0:NB]
            p_t = bank[0][:, 0:GE * ET]
            p_h = p_t
            p_tz = bank[0][:, 512:512 + ET]
            p_w = bank[1][0:ET, :].rearrange("p (t c) -> p t c", c=TS)[:, :, 0:W]
            p_x = bank[2][0:ET, :].rearrange("p (t c) -> p t c", c=TS)[:, :, 0:F]
            p_xs = p_x[:, :, 0:S]
            p_xv = p_x[:, :, S:F].rearrange("p t (i k) -> p t i k", i=3)
            p_m = bank[3][0:ET, 0:2 * Z].rearrange("p (t c) -> p t c", c=Z)
            p_tt = bank[3][:, 512:512 + 4 * ET]
            q_t = [bank[0][:, 0:512], bank[0][:, 512:1024]]
            q_tz = [bank[1][:, 0:P], bank[1][:, 512:512 + P]]
            q_z = [bank[2 + h][:, :].rearrange("p (t c) -> p t c", c=TS) for h in range(2)]

            block = psum_ctx.enter_context(nc.Block())

            @block.sync
            def _(sp):
                sp.dma_start(src_i[:], src).then_inc(s_in, 16)
                sp.dma_start(dst_i[:], dst).then_inc(s_in, 16)
                sp.dma_start(vec[:], edge_vec).then_inc(s_in, 16)
                sp.dma_start(wfc2[:], w_fc2).then_inc(s_w, 16)
                sp.dma_start(wos[:], w_out_s).then_inc(s_w, 16)
                sp.dma_start(wov[:], w_out_v).then_inc(s_w, 16)
                sp.wait_ge(s_clr, 1)
                sp.dma_start(wfc1[:, 0:EF], w_fc1).then_inc(s_w, 16)
                sp.dma_start(wsk_a[0:S, 0:SG], w_skip0).then_inc(s_w, 16)
                sp.dma_start(wnl_a[0:S, 0:S], w_nl0).then_inc(s_w, 16)
                for j in range(2):
                    rows = slice(S + V * j, S + V * j + V)
                    sp.dma_start(wsk_a[rows, SG + V * j:SG + V * j + V], w_skip1).then_inc(s_w, 16)
                    sp.dma_start(wnl_a[rows, S + V * j:S + V * j + V], w_nl1).then_inc(s_w, 16)
                for j in range(4):
                    cols = slice(V * j, V * j + V)
                    sp.dma_start(wsk_z[j:P:4, cols], w_skip1).then_inc(s_w, 16)
                    sp.dma_start(wnl_z[j:P:4, cols], w_nl1).then_inc(s_w, 16)
                sp.dma_start(messages[0:1, :], row0[:, :]).then_inc(s_row0, 16)

                def store_msgs(p, b):
                    sp.wait_ge(e_msb, 2 * p + 2)
                    rows = messages[bass.ds(p * (GE * ET) + 1, GE * ET), :]
                    sp.dma_start(rows.rearrange("(t p) c -> p t c", p=ET), msg[:, b, :, :]).then_inc(e_st[b], 16)

                def load_f(q, c):
                    wait(sp, e_h1, q - 1)
                    sp.dma_start(ef[:, c, :], edge_feat_t[:, bass.ds(q * (GE * ET), GE * ET)]).then_inc(e_f[c], 16)

                load_f(0, 0)

                def round_e(q, b):
                    if within(q + 1):
                        load_f(q + 1, 1 - b % 2)
                    if within(q - 3):
                        store_msgs(q - 3, 1 - b % 2)

                groups(sp, round_e)

                def nodes(n, every):
                    def load_x(i, u):
                        rows = x[bass.ds(i * MN, MN), :].rearrange("(p g) f -> p g f", g=G)
                        sp.dma_start(xb[:, u, :, :], rows).then_inc(n.x[u], 16)

                    def load_last(u):
                        rows = x[(NM - 1) * MN:N, :].rearrange("(p g) f -> p g f", g=G)
                        sp.dma_start(xb[0:LAST_P, u, :, :], rows).then_inc(n.x[u], 16)

                    def store_o(i, u):
                        sp.wait_ge(n.res[0], i + 1)
                        sp.wait_ge(n.res[1], i + 1)
                        if isinstance(i, int) and i == NM - 1:
                            rows = out[(NM - 1) * MN:N, :].rearrange("(p g) f -> p g f", g=G)
                            sp.dma_start(rows, ob[0:LAST_P, u, :, :]).then_inc(n.st[u], 16)
                        else:
                            rows = out[bass.ds(i * MN, MN), :].rearrange("(p g) f -> p g f", g=G)
                            sp.dma_start(rows, ob[:, u, :, :]).then_inc(n.st[u], 16)

                    load_x(0, 0)
                    load_x(1, 1)
                    load_x(2, 2)

                    def round_n(i, u):
                        if macro_exists(i - 1):
                            store_o(i - 1, (u + 3) % U)
                        if isinstance(i, int) and i + 3 == NM - 1:
                            load_last((u + 3) % U)
                        elif macro_exists(i + 3):
                            load_x(i + 3, (u + 3) % U)
                        if every:
                            def chunk(k, b):
                                sp.wait_ge(r_used, RC * (i * NC + k - 1) + CREDIT)
                                rows = messages[bass.ds(k * (RC * ET) + 1, RC * ET), :]
                                sp.dma_start(again[:, b, :, :], rows.rearrange("(t p) c -> p t c", p=ET)
                                             ).then_inc(r_m[b], 16)

                            chunks(sp, chunk)

                    macros(sp, round_n)
                    store_o(NM - 1, (NM - 1) % U)
                    for u in range(U):
                        sp.wait_ge(n.st[u], 16 * len(range(u, NM, U)))

                nodes(main, False)
                sp.wait_ge(b_fin, 1)
                with sp.If(sp.value_load(most_i[0:1, 0:1]) > CAP):
                    nodes(redo, True)

            @block.gpsimd
            def _(pool):
                pool.memset(neg_half[:], -0.5).then_inc(s_const, 1)
                pool.memset(half_nt[:], -0.5).then_inc(s_const, 1)
                pool.memset(ident[:], 0.0).then_inc(s_pc, 1)
                pool.memset(tri_before[:], 0.0).then_inc(s_pc, 1)
                pool.memset(tri_rest[:], 0.0).then_inc(s_pc, 1)
                pool.iota(iota_i[:], pattern=[[1, 512]], base=0, channel_multiplier=0).then_inc(s_const, 1)
                pool.iota(num_i[:], pattern=[[ET, NT]], base=1, channel_multiplier=1).then_inc(s_const, 1)
                pool.wait_ge(s_pc, 3)
                pool.affine_select(out=ident[:], in_=ident[:], compare_op=ALU.not_equal, fill=1.0, base=0,
                                   pattern=[[-1, P]], channel_multiplier=1).then_inc(s_const, 1)
                pool.affine_select(out=tri_before[:], in_=tri_before[:], compare_op=ALU.is_ge, fill=1.0, base=0,
                                   pattern=[[-1, ET]], channel_multiplier=1).then_inc(s_const, 1)
                pool.affine_select(out=tri_rest[:], in_=tri_rest[:], compare_op=ALU.is_gt, fill=1.0, base=0,
                                   pattern=[[1, ET]], channel_multiplier=-1).then_inc(s_const, 1)
                pool.wait_ge(s_const, 7)
                pool.wait_ge(s_tab, 1)
                pool.tensor_tensor(vec_r[:], vec_d2[:], half_nt[:], ALU.pow).then_inc(s_r, 1)

                def gathers(q, b):
                    wait(pool, e_norm, q - D + 1)
                    pool.tensor_copy(dst_g[:, b, :], dst_i[:, bass.ds(q * GE, GE)]).then_inc(e_idx, 1)
                    pool.wait_ge(e_idx, q + 1)
                    pool.sem_inc(s_held, 1)
                    for t in range(GE):
                        pool.indirect_dma_start(xg[:, b, t, :], None, x[:, :],
                                                bass.IndirectOffsetOnAxis(ap=dst_g[:, b, t:t + 1], axis=0)
                                                ).then_inc(e_x[b], 16)

                def scales(q, b):
                    pool.wait_ge(e_var, q + 1)
                    pool.tensor_tensor(e_rstd[:, b, :], e_sum[:, b, 4, :], neg_half[0:ET, 0:GE], ALU.pow).then_inc(e_pw, 1)
                    pool.wait_ge(e_pw, q + 1)
                    pool.tensor_tensor(e_bias[:, b, :], e_sum[:, b, 2, :], e_rstd[:, b, :], ALU.mult).then_inc(e_ln, 1)

                pool.wait_ge(s_in, 48)
                for q in range(3):
                    gathers(q, q)
                scales(0, 0)
                scales(1, 1)

                def round_e(q, b):
                    if within(q + 3):
                        gathers(q + 3, (b + 3) % D)
                    if within(q + 2):
                        scales(q + 2, (b + 2) % D)
                    if within(q - 1):
                        p = q - 1
                        h = hat[:, bass.ds(p * GE, GE), :]
                        pool.wait_ge(e_t1, p + 1)
                        wait(pool, e_tp, p)
                        pool.tensor_tensor(cr_a[:, :, 0:2, :], w4xv[:, :, 1:3, :],
                                           h[:, :, 2:4].unsqueeze(3).to_broadcast((ET, GE, 2, V)), ALU.mult)
                        pool.tensor_tensor(cr_a[:, :, 2, :], w4xv[:, :, 0, :],
                                           h[:, :, 1:2].to_broadcast((ET, GE, V)), ALU.mult).then_inc(e_gp, 1)

                groups(pool, round_e)

                def nodes(n, every):
                    def fetch(i, u):
                        wait(pool, n.z, 2 * (i - U) + 2)
                        pool.tensor_copy(slot_m[:, u, :], slots_i[:, bass.ds(i * BPM, BPM)]).then_inc(n.idx, 1)
                        pool.wait_ge(n.idx, i + 1)
                        pool.sem_inc(s_held, 1)
                        for k in range(BPM):
                            pool.indirect_dma_start(mg[:, u, k, :], None, messages[:, :],
                                                    bass.IndirectOffsetOnAxis(ap=slot_m[:, u, k:k + 1], axis=0)
                                                    ).then_inc(n.g[u], 16)

                    def ln_n(i, u):
                        pool.wait_ge(n.var, i + 1)
                        pool.tensor_tensor(n_rstd[:, u, :], n_sum[:, u, 4, :], neg_half[:, :], ALU.pow).then_inc(n.pw, 1)
                        pool.wait_ge(n.pw, i + 1)
                        pool.tensor_tensor(n_bias[:, u, :], n_sum[:, u, 2, :], n_rstd[:, u, :], ALU.mult).then_inc(n.ln, 1)

                    if not every:
                        fetch(0, 0)
                        fetch(1, 1)
                    ln_n(0, 0)
                    ln_n(1, 1)

                    def residual(i, u):
                        pool.wait_ge(n.mul, 2 * i + 1)
                        pool.tensor_tensor(ob[:, u, 0:RP, :], ob[:, u, 0:RP, :], xb[:, u, 0:RP, :], ALU.add).then_inc(n.res[0], 1)

                    def round_n(i, u):
                        if macro_exists(i - 1):
                            residual(i - 1, (u + 3) % U)
                        if macro_exists(i + 2):
                            if not every:
                                fetch(i + 2, (u + 2) % U)
                            ln_n(i + 2, (u + 2) % U)

                    macros(pool, round_n)
                    residual(NM - 1, (NM - 1) % U)

                pool.wait_ge(b_fin, 1)
                pool.wait_ge(s_row0, 16)
                pool.wait_ge(e_st[0], 16 * (NG // 2))
                pool.wait_ge(e_st[1], 16 * (NG // 2))
                nodes(main, False)
                pool.wait_ge(b_fin, 1)
                with pool.If(pool.value_load(most_i[0:1, 0:1]) > CAP):
                    pool.iota(iota_i[:], pattern=[[1, 4], [G, P]], base=0, channel_multiplier=0).then_inc(r_iota, 1)
                    nodes(redo, True)

            @block.vector
            def _(dve):
                steps = [0]

                def link(ins):
                    steps[0] += 1
                    ins.then_inc(s_dc, 1)
                    dve.wait_ge(s_dc, steps[0])

                for t in (wfc1, wsk_a, wsk_z, wnl_a, wnl_z, msg, tp_s, row0, zeros_w):
                    last = dve.memset(t[:], 0.0)
                link(last)
                link(dve.memset(row0[:, LOCAL:LOCAL + 1], -1.0))
                dve.memset(ones_bf[:], 1.0)
                dve.memset(zeros_bf[:], 0.0).then_inc(s_clr, 1)
                dve.wait_ge(s_in, 48)
                dve.wait_ge(s_const, 7)
                link(dve.tensor_tensor(vec_sq[:], vec[:], vec[:], ALU.mult))
                link(dve.tensor_tensor(vec_d2[:], vec_sq[:, :, 0], vec_sq[:, :, 1], ALU.add))
                dve.tensor_tensor(vec_d2[:], vec_d2[:], vec_sq[:, :, 2], ALU.add).then_inc(s_tab, 1)
                dve.tensor_copy(iota_bin[:], iota_i[:, 0:NB])
                dve.tensor_copy(iota_slot[:], iota_i[:, 0:CAP])
                dve.tensor_copy(iota_local[:], iota_i[:, 0:2 * P])
                link(dve.tensor_scalar(tmp_a[:], src_i[:], 10, 2, ALU.logical_shift_right, ALU.logical_shift_left))
                link(dve.tensor_scalar(tmp_b[:], src_i[:], 1, BPM - 1, ALU.logical_shift_right, ALU.bitwise_and))
                link(dve.tensor_tensor(bin_of[:], tmp_a[:], tmp_b[:], ALU.add))
                link(dve.tensor_scalar(tmp_a[:], src_i[:], 3, P - 1, ALU.logical_shift_right, ALU.bitwise_and))
                link(dve.tensor_scalar(tmp_b[:], src_i[:], 1, 7, ALU.bitwise_and, ALU.logical_shift_left))
                link(dve.tensor_tensor(place_of[:, :, 0], tmp_a[:], tmp_b[:], ALU.add))
                dve.tensor_copy(place_of[:, :, 1], src_i[:])
                link(dve.tensor_scalar(tmp_a[:], num_i[:], 7, None, ALU.logical_shift_right))
                link(dve.tensor_scalar(tmp_b[:], num_i[:], P - 1, None, ALU.bitwise_and))
                link(dve.tensor_copy(num_hi[:], tmp_a[:]))
                link(dve.tensor_copy(num_lo[:], tmp_b[:]))
                link(dve.tensor_scalar(neg_hi[:], num_hi[:], -1.0, None, ALU.mult))
                dve.memset(most[:], 0.0)
                dve.tensor_scalar(neg_lo[:], num_lo[:], -1.0, None, ALU.mult).then_inc(b_const, 1)

                def bins_of(t, k):
                    wait(dve, b_tab, t - BR + 1)
                    dve.tensor_scalar(bin_hot[:, k, :], iota_bin[0:ET, :], bin_of[:, bass.ds(t, 1)], None,
                                      ALU.is_equal).then_inc(b_hot, 1)

                for t in range(4):
                    bins_of(t, t)

                def tile_b(t, k):
                    wait(dve, b_rank, t - 1)
                    dve.wait_ge(b_pre, t + 1)
                    dve.tensor_tensor_reduce(out=rank_junk[:, k % 2, :], in0=bin_hot[:, k, :], in1=p_cnt[k % 2], scale=1.0,
                                             scalar=0.0, op0=ALU.mult, op1=ALU.add,
                                             accum_out=rank[:, k:k + 1]).then_inc(b_rank, 1)
                    if tile_exists(t + 4):
                        bins_of(t + 4, (k + 4) % BR)

                edge_tiles(dve, tile_b)
                dve.wait_ge(b_end, 1)
                dve.reduce_max(most[:], p_cnt[(NT - 1) % 2], AX_X).then_inc(b_most, 1)
                dve.wait_ge(b_most, 1)
                dve.tensor_copy(most_i[:], most[:])
                dve.wait_ge(b_lo, 1)
                dve.scalar_tensor_tensor(out=slots_i[:], in0=p_hi, scalar=float(P), in1=tab_lo[:],
                                         op0=ALU.mult, op1=ALU.add).then_inc(b_fin, 1)
                dve.wait_ge(s_r, 1)
                link(dve.tensor_tensor(hat[:, :, 0:3], vec[:], vec_r[:, :].unsqueeze(2).to_broadcast((ET, NT, 3)), ALU.mult))
                dve.tensor_copy(hat[:, :, 3], hat[:, :, 0]).then_inc(s_tab, 1)
                dve.wait_ge(s_tab, 2)
                dve.wait_ge(s_w, 16 * 18)
                dve.tensor_scalar(wos[:], wos[:], 1.0 / 32.0, None, ALU.mult)
                dve.tensor_scalar(wov[0:64, :], wov[0:64, :], 3.0 ** 0.5 / 32.0, None, ALU.mult)
                dve.tensor_scalar(wov[64:96, :], wov[64:96, :], 1.0 / 32.0, None, ALU.mult)
                dve.tensor_scalar(wov[96:128, :], wov[96:128, :], 1.5 ** 0.5 / 32.0, None, ALU.mult).then_inc(s_wready, 1)

                def layer_norm(rows, stat, sums, chain, base, done, meanwhile=(None, None)):
                    for t in range(rows.shape[1]):
                        last = dve.bn_stats(stat[:, t, :], rows[:, t, :])
                    last.then_inc(chain, 1)
                    dve.wait_ge(chain, base + 1)
                    dve.tensor_tensor(sums[:, 0, :], stat[:, :, 1], stat[:, :, 4], ALU.subtract)
                    dve.tensor_tensor(sums[:, 1, :], stat[:, :, 2], stat[:, :, 5], ALU.add)
                    dve.tensor_tensor(sums[:, 2, :], stat[:, :, 1], stat[:, :, 4], ALU.add).then_inc(chain, 1)
                    if meanwhile[0]:
                        meanwhile[0]()
                    dve.wait_ge(chain, base + 2)
                    dve.tensor_tensor(sums[:, 3, :], sums[:, 0, :], sums[:, 0, :], ALU.mult)
                    dve.tensor_scalar(sums[:, 1, :], sums[:, 1, :], 1.0 / F, EPS, ALU.mult, ALU.add)
                    dve.tensor_scalar(sums[:, 2, :], sums[:, 2, :], -0.5, None, ALU.mult).then_inc(chain, 1)
                    if meanwhile[1]:
                        meanwhile[1]()
                    dve.wait_ge(chain, base + 3)
                    dve.scalar_tensor_tensor(out=sums[:, 4, :], in0=sums[:, 3, :], scalar=0.25,
                                             in1=sums[:, 1, :], op0=ALU.mult, op1=ALU.add).then_inc(done, 1)

                def stats_e(q, b):
                    dve.wait_ge(e_x[b], earlier(q, b, D, 64) + 64)
                    wait(dve, e_norm, q - D + 1)
                    layer_norm(xg[:, b, :, :], e_stat[:, b, :, :], e_sum[:, b, :, :], e_c, 3 * q, e_var)

                def products(p, c):
                    w = w_sb[:, c, :, :]
                    h3 = hat[:, bass.ds(p * GE, GE), 0:3].unsqueeze(3)
                    h = hat[:, bass.ds(p * GE, GE), :]
                    dve.wait_ge(e_wsb, p + 1)
                    dve.wait_ge(e_xs, p + 1)
                    wait(dve, e_gp, p)
                    wait(dve, e_tp, p)
                    wait(dve, e_tt, GE * (p - 1))
                    dve.tensor_tensor(w4xv[:], w[:, :, W - V:W].unsqueeze(2).to_broadcast((ET, GE, 3, V)),
                                      p_xv, ALU.mult).then_inc(e_t1, 1)
                    dve.tensor_tensor(w1xs[:], w[:, :, S:2 * S], p_xs, ALU.mult).then_inc(e_c4, 1)
                    dve.tensor_tensor(xvh[:], h3.to_broadcast((ET, GE, 3, V)), p_xv, ALU.mult).then_inc(e_c2, 1)
                    dve.tensor_tensor(tp_s[:, c, :, 0:S], w[:, :, 0:S], p_xs, ALU.mult)
                    dve.tensor_tensor(tp_v[:, c, :, :, S:S + V],
                                      w[:, :, 2 * S:2 * S + V].unsqueeze(2).to_broadcast((ET, GE, 3, V)),
                                      p_xv, ALU.mult).then_inc(e_px, 1)
                    dve.wait_ge(e_c2, 3 * p + 1)
                    dve.tensor_tensor(dot[:, 0, :, :], xvh[:, :, 0, :], xvh[:, :, 1, :], ALU.add).then_inc(e_c2, 1)
                    dve.wait_ge(e_t1, p + 1)
                    dve.tensor_tensor(cr_b[:, :, 0, :], w4xv[:, :, 2, :], h[:, :, 1:2].to_broadcast((ET, GE, V)), ALU.mult)
                    dve.wait_ge(e_c2, 3 * p + 2)
                    dve.tensor_tensor(dot[:, 1, :, :], dot[:, 0, :, :], xvh[:, :, 2, :], ALU.add).then_inc(e_c2, 1)
                    dve.tensor_tensor(cr_b[:, :, 1:3, :], w4xv[:, :, 0:2, :],
                                      h[:, :, 2:4].unsqueeze(3).to_broadcast((ET, GE, 2, V)), ALU.mult).then_inc(e_c3, 1)
                    dve.wait_ge(e_c4, p + 1)
                    dve.tensor_tensor(tp_v[:, c, :, :, 0:S],
                                      w1xs[:, :, :].unsqueeze(2).to_broadcast((ET, GE, 3, S)),
                                      h3.to_broadcast((ET, GE, 3, S)), ALU.mult)
                    dve.wait_ge(e_c2, 3 * p + 3)
                    dve.tensor_tensor(tp_s[:, c, :, S:SG], dot[:, 1, :, :], w[:, :, 2 * S + V:2 * S + 2 * V], ALU.mult)
                    dve.wait_ge(e_c3, p + 1)
                    dve.wait_ge(e_gp, p + 1)
                    wait(dve, e_st[c], earlier(p, c, 2, 16))
                    dve.tensor_copy(msg[:, c, :, LOCAL:NODE + 1], place_of[:, bass.ds(p * GE, GE), :])
                    dve.tensor_tensor(tp_v[:, c, :, :, S + V:P], cr_a[:], cr_b[:], ALU.subtract).then_inc(e_tp, 1)

                stats_e(0, 0)
                stats_e(1, 1)

                def round_e(q, b):
                    if within(q + 2):
                        stats_e(q + 2, (b + 2) % D)
                    if within(q - 1):
                        products(q - 1, (b + 1) % 2)

                groups(dve, round_e)

                def nodes(n, every):
                    def stats_n(i, u, meanwhile=(None, None)):
                        dve.wait_ge(n.x[u], earlier(i, u, U, 16) + 16)
                        wait(dve, n.norm, 2 * (i - U) + 2)
                        layer_norm(xb[:, u, :, :], n_stat[:, u, :, :], n_sum[:, u, :, :], n.c, 3 * i, n.var,
                                   meanwhile)

                    def hot_n(i, u, bins=range(BPM)):
                        if 0 in bins:
                            dve.wait_ge(n.g[u], earlier(i, u, U, 64) + 64)
                            wait(dve, n.z, 2 * (i - 2) + 2)
                        for k in bins:
                            last = dve.tensor_scalar(hot[:, u % 2, k, :], iota_local[:], mg[:, u, k, LOCAL:LOCAL + 1],
                                                     None, ALU.is_equal)
                        if BPM - 1 in bins:
                            last.then_inc(n.hot, 1)

                    def gate(i, u, h):
                        if h == 0:
                            wait(dve, n.st[u], earlier(i, u, U, 16))
                        dve.wait_ge(n.sg, 2 * i + h + 1)
                        z = q_z[h]
                        o = ob[:, u, 4 * h:4 * h + 4, :]
                        dve.tensor_tensor(o[:, :, 0:S], z[:, :, 0:S], sg[:, h, :, 0:S], ALU.mult)
                        dve.tensor_tensor(o[:, :, S:F].rearrange("p t (i k) -> p t i k", i=3),
                                          z[:, :, SG:Z].rearrange("p t (i k) -> p t i k", i=3),
                                          sg[:, h, :, S:SG].unsqueeze(2).to_broadcast((P, 4, 3, V)),
                                          ALU.mult).then_inc(n.mul, 1)

                    def residual(i, u):
                        dve.wait_ge(n.mul, 2 * i + 2)
                        dve.tensor_tensor(ob[:, u, RP:G, :], ob[:, u, RP:G, :], xb[:, u, RP:G, :], ALU.add).then_inc(n.res[1], 1)

                    def places(i):
                        def chunk(k, b):
                            c = i * NC + k
                            dve.wait_ge(r_m[b], (c + (2 if b == 0 else 1)) // 2 * 16 if isinstance(c, int)
                                        else (c + (2 if b == 0 else 1)) * 8)
                            dve.tensor_scalar(rel[:, b, :], again[:, b, :, NODE], macro_base[:, :], None,
                                              ALU.subtract).then_inc(r_rel, 1)
                            dve.wait_ge(r_rel, c + 1)
                            for t in range(RC):
                                m = c * RC + t
                                dve.wait_ge(r_used, m - 1 + CREDIT)
                                dve.tensor_scalar(key_hot[:, t % 2, :], iota_key[:], rel[:, b, t:t + 1], None,
                                                  ALU.is_equal).then_inc(n.hot, 1)

                        chunks(dve, chunk)
                        dve.tensor_scalar(macro_base[:], macro_base[:], float(MN), None, ALU.add).then_inc(r_base, 1)
                        dve.wait_ge(r_base, i + 1)

                    stats_n(0, 0)
                    stats_n(1, 1)
                    if not every:
                        hot_n(0, 0)

                    def round_n(i, u):
                        if macro_exists(i - 1):
                            gate(i - 1, (u + 3) % U, 1)
                            residual(i - 1, (u + 3) % U)
                        if macro_exists(i + 1) and not every:
                            hots = [lambda b=b: hot_n(i + 1, (u + 1) % U, b) for b in (range(0, 2), range(2, 4))]
                        else:
                            hots = [None, None]
                        if macro_exists(i + 2):
                            stats_n(i + 2, (u + 2) % U, hots)
                        else:
                            for h in hots:
                                if h:
                                    h()
                        if every:
                            places(i)
                        gate(i, u, 0)

                    macros(dve, round_n)
                    gate(NM - 1, (NM - 1) % U, 1)
                    residual(NM - 1, (NM - 1) % U)

                nodes(main, False)
                dve.wait_ge(b_fin, 1)
                with dve.If(dve.value_load(most_i[0:1, 0:1]) > CAP):
                    dve.wait_ge(r_iota, 1)
                    for g in range(2):
                        dve.tensor_scalar(iota_key[:, 512 * g:512 * g + 512], iota_i[0:ET, :], float(4 * g), None, ALU.add)
                    dve.memset(macro_base[:], 0.0).then_inc(r_key, 1)
                    dve.wait_ge(r_key, 1)
                    nodes(redo, True)

            @block.scalar
            def _(act):
                act.wait_ge(b_const, 1)

                def slots_of(t, k):
                    act.activation(slot_hi[:, k % GE, :], off_slot[:, k % GE, :], ACT.Relu,
                                   bias=num_hi[:, bass.ds(t, 1)], scale=neg_hi[:, bass.ds(t, 1)])
                    act.activation(slot_lo[:, k % GE, :], off_slot[:, k % GE, :], ACT.Relu,
                                   bias=num_lo[:, bass.ds(t, 1)], scale=neg_lo[:, bass.ds(t, 1)]).then_inc(b_slot, 1)

                def tile_b(t, k):
                    wait(act, b_tab, t - GE + 1)
                    wait(act, b_off, t)
                    act.wait_ge(b_rank, t + 1)
                    act.activation(off_slot[:, k % GE, :], iota_slot[0:ET, :], ACT.Abs, bias=rank[:, k:k + 1],
                                   scale=-1.0).then_inc(b_off, 1)
                    if tile_exists(t - 1):
                        slots_of(t - 1, (k - 1) % BR)

                edge_tiles(act, tile_b)
                act.wait_ge(b_off, NT)
                slots_of(NT - 1, (NT - 1) % BR)
                act.wait_ge(b_end, 1)
                act.activation(tab_lo[:], p_lo, ACT.Copy).then_inc(b_lo, 1)

                def norm_e(q, b, tiles):
                    act.wait_ge(e_ln, q + 1)
                    wait(act, e_t, q - 1)
                    for t in tiles:
                        last = act.activation(hn[:, b % 2, :, t], xg[:, b, t, :], ACT.Relu,
                                              bias=e_bias[:, b, t:t + 1], scale=e_rstd[:, b, t:t + 1])
                    if GE - 1 in tiles:
                        last.then_inc(e_norm, 1)

                norm_e(0, 0, range(GE))

                def round_e(q, b):
                    c = b % 2

                    def take(t):
                        p = q - 2
                        if within(p):
                            act.wait_ge(e_tt, GE * p + t + 1)
                            wait(act, e_m, GE * p + t - 1)
                            act.activation(tpt[:, t % 2, :], p_tt, ACT.Copy).then_inc(e_ttsb, 1)

                    def put(p, c, j):
                        if within(p):
                            act.wait_ge(e_m, GE * p + 2 * j + 2)
                            if j == 0:
                                wait(act, e_st[c], earlier(p, c, 2, 16))
                            act.activation(msg[:, c, 2 * j:2 * j + 2, 0:Z], p_m, ACT.Copy).then_inc(e_msb, 1)

                    if within(q):
                        act.wait_ge(e_t, q + 1)
                        wait(act, e_xs, q - 1)
                        act.activation(ht[:, c, :], p_t, ACT.Copy)
                        act.activation(hz[:, c, :], p_tz, ACT.Copy).then_inc(e_ht, 1)
                    put(q - 3, 1 - c, 1)
                    take(0)
                    if within(q):
                        act.wait_ge(e_h1, q + 1)
                        wait(act, e_w, q)
                        act.activation(hid[:], p_h[0:EF, :], ACT.Relu).then_inc(e_hid, 1)
                    take(1)
                    if within(q + 1):
                        norm_e(q + 1, (b + 1) % D, range(0, 2))
                    take(2)
                    put(q - 2, c, 0)
                    if within(q + 1):
                        norm_e(q + 1, (b + 1) % D, range(2, 4))
                    take(3)
                    if within(q):
                        act.wait_ge(e_w, q + 1)
                        wait(act, e_tp, q - 1)
                        act.activation(w_sb[:, c, :, :], p_w, ACT.Copy).then_inc(e_wsb, 1)

                groups(act, round_e)

                def nodes(n, every):
                    def norm(i, u, h):
                        act.wait_ge(n.ln, i + 1)
                        wait(act, n.t, 2 * (i - 2) + h + 1)
                        for g in range(4 * h, 4 * h + 4):
                            last = act.activation(nn[:, u % 2, h, :, g % 4], xb[:, u, g, :], ACT.Relu,
                                                  bias=n_bias[:, u, g:g + 1], scale=n_rstd[:, u, g:g + 1])
                        last.then_inc(n.norm, 1)

                    def evacuate(i, h):
                        act.wait_ge(n.t, 2 * i + h + 1)
                        wait(act, n.z, 2 * i + h - 1)
                        act.activation(nt_a[:, h, :], q_t[h], ACT.Copy)
                        act.activation(nt_z[:, h, :], q_tz[h], ACT.Copy).then_inc(n.ht, 1)

                    def sigmoids(i, h):
                        act.wait_ge(n.z, 2 * i + h + 1)
                        wait(act, n.mul, 2 * i + h - 1)
                        act.activation(sg[:, h, :, :], q_z[h][:, :, 0:SG], ACT.Sigmoid).then_inc(n.sg, 1)

                    norm(0, 0, 0)
                    norm(0, 0, 1)
                    evacuate(0, 0)

                    def round_n(i, u):
                        if macro_exists(i - 1):
                            sigmoids(i - 1, 1)
                        evacuate(i, 1)
                        if macro_exists(i + 1):
                            norm(i + 1, (u + 1) % U, 0)
                        sigmoids(i, 0)
                        if macro_exists(i + 1):
                            evacuate(i + 1, 0)
                            norm(i + 1, (u + 1) % U, 1)

                    macros(act, round_n)
                    sigmoids(NM - 1, 1)

                nodes(main, False)
                act.wait_ge(b_fin, 1)
                with act.If(act.value_load(most_i[0:1, 0:1]) > CAP):
                    nodes(redo, True)

            @block.tensor
            def _(pe):
                pe.wait_ge(b_hot, 1)
                for o in (p_cnt[0], p_cnt[1], p_hi, p_lo):
                    pe.matmul(o, zeros_bf[0:ET, 0:o.shape[0]], zeros_bf[0:ET, :], start=True, stop=False,
                              skip_group_check=True)

                def count(k, tri, of):
                    return pe.matmul(p_cnt[k % 2], tri[:], bin_hot[:, of % BR, :], start=False, stop=False,
                                     skip_group_check=True)

                def table(t, k):
                    pe.wait_ge(b_slot, t + 1)
                    for o, slot in ((p_hi, slot_hi), (p_lo, slot_lo)):
                        last = pe.matmul(o, slot[:, k % GE, :], bin_hot[:, k, :], start=False, stop=False,
                                         skip_group_check=True)
                    last.then_inc(b_tab, 1)

                count(0, tri_before, 0).then_inc(b_pre, 1)
                pe.wait_ge(b_hot, 2)
                count(1, ones_bf, 0)
                count(1, tri_before, 1).then_inc(b_pre, 1)

                def tile_b(t, k):
                    if tile_exists(t + 2):
                        pe.wait_ge(b_hot, t + 3)
                    pe.wait_ge(b_rank, t + 1)
                    count(k, tri_rest, k)
                    if tile_exists(t + 2):
                        count(k, ones_bf, k + 1)
                        count(k, tri_before, k + 2).then_inc(b_pre, 1)
                    if tile_exists(t - 2):
                        table(t - 2, (k - 2) % BR)

                edge_tiles(pe, tile_b)
                table(NT - 2, (NT - 2) % BR)
                table(NT - 1, (NT - 1) % BR)
                for o in (p_cnt[0], p_cnt[1], p_hi, p_lo):
                    last = pe.matmul(o, zeros_bf[0:ET, 0:o.shape[0]], zeros_bf[0:ET, :], start=False, stop=True,
                                     skip_group_check=True)
                last.then_inc(b_end, 1)
                pe.wait_ge(b_fin, 1)
                pe.wait_ge(s_wready, 1)

                idt = ident[0:ET, 0:ET]

                def turn_rows(q, c):
                    pe.wait_ge(e_norm, q + 1)
                    wait(pe, e_ht, q)
                    wait(pe, e_hid, q)
                    for t in range(GE):
                        pe.transpose(p_t[:, t * ET:(t + 1) * ET], hn[:, c, 0:P, t], idt)
                    pe.transpose(p_tz, hn[:, c, P:F, :], idt).then_inc(e_t, 1)

                turn_rows(0, 0)

                def round_e(q, b):
                    p, c = q - 2, b % 2

                    def turn(t):
                        if not within(p):
                            return
                        if t == 0:
                            pe.wait_ge(e_tp, p + 1)
                        wait(pe, e_ttsb, GE * p + t)
                        pe.transpose(p_tt[:, 0:ET], tp_s[:, c, t, :], idt)
                        for i in range(3):
                            last = pe.transpose(p_tt[:, (i + 1) * ET:(i + 2) * ET], tp_v[:, c, t, i, :], idt)
                        last.then_inc(e_tt, 1)

                    def project(t):
                        if not within(p):
                            return
                        pe.wait_ge(e_ttsb, GE * p + t + 1)
                        if t % 2 == 0:
                            wait(pe, e_msb, 2 * p + t // 2)
                        a = tpt[:, t % 2, :]
                        pe.matmul(p_m[:, t % 2, 0:SG], a[0:SG, 0:ET], wos[:], start=(t % 2 == 0), stop=True,
                                  skip_group_check=True)
                        for i in range(3):
                            last = pe.matmul(p_m[:, t % 2, SG + V * i:SG + V * i + V],
                                             a[:, (i + 1) * ET:(i + 2) * ET], wov[:], start=False, stop=True,
                                             skip_group_check=True)
                        last.then_inc(e_m, 1)

                    def weights(tiles):
                        if not within(q):
                            return
                        if 0 in tiles:
                            pe.wait_ge(e_hid, q + 1)
                            wait(pe, e_wsb, q)
                        for t in tiles:
                            last = pe.matmul(p_w[:, t, :], hid[:, t * ET:(t + 1) * ET], wfc2[:], start=True, stop=True)
                        if GE - 1 in tiles:
                            last.then_inc(e_w, 1)

                    turn(0)
                    if within(q):
                        pe.wait_ge(e_f[c], earlier(q, c, 2, 16) + 16)
                        pe.wait_ge(e_ht, q + 1)
                        pe.matmul(p_h, wfc1[:], ef[:, c, :], start=True, stop=True).then_inc(e_h1, 1)
                    turn(1)
                    project(0)
                    weights((0, 1))
                    turn(2)
                    project(1)
                    weights((2, 3))
                    turn(3)
                    project(2)
                    if within(q + 1):
                        turn_rows(q + 1, 1 - c)
                    project(3)
                    if within(q):
                        wait(pe, e_px, q)
                        for t in range(GE):
                            pe.matmul(p_x[:, t, 0:P], ht[:, c, t * ET:(t + 1) * ET], wnl_a[:],
                                      start=(t % 2 == 0), stop=True, skip_group_check=True)
                        for j in range(2):
                            last = pe.matmul(p_x[:, 2 * j:2 * j + 2, P:F], hz[:, c, :],
                                             wnl_z[:, 2 * V * j:2 * V * j + 2 * V],
                                             start=False, stop=True, skip_group_check=True)
                        last.then_inc(e_xs, 1)

                groups(pe, round_e)
                pe.wait_ge(e_msb, 2 * NG)

                def nodes(n, every):
                    def turn(i, u, h):
                        pe.wait_ge(n.norm, 2 * i + h + 1)
                        wait(pe, n.ht, 2 * i + h - 1)
                        for t in range(4):
                            pe.transpose(q_t[h][:, t * P:(t + 1) * P], nn[:, u % 2, h, 0:P, t], ident[:])
                        pe.transpose(q_tz[h], nn[:, u % 2, h, P:F, :], ident[:]).then_inc(n.t, 1)

                    def skip(i, h):
                        z = q_z[h]
                        pe.wait_ge(n.ht, 2 * i + h + 1)
                        wait(pe, n.mul, 2 * i + h - 1)
                        for t in range(4):
                            pe.matmul(z[:, t, 0:F], nt_a[:, h, t * P:(t + 1) * P], wsk_a[:], start=(t % 2 == 0),
                                      stop=False, skip_group_check=True)
                        for j in range(2):
                            last = pe.matmul(z[:, 2 * j:2 * j + 2, F:Z], nt_z[:, h, :],
                                             wsk_z[:, 2 * V * j:2 * V * j + 2 * V],
                                             start=False, stop=every, skip_group_check=True)
                        return last

                    def add(i, u, h):
                        if h == 0:
                            pe.wait_ge(n.hot, i + 1)
                        for t in range(4):
                            g = 4 * h + t
                            last = pe.matmul(q_z[h][:, t, 0:Z], hot[:, u % 2, g // 2, (g % 2) * P:(g % 2) * P + P],
                                             mg[:, u, g // 2, 0:Z], start=False, stop=True, skip_group_check=True)
                        last.then_inc(n.z, 1)

                    def add_every(i):
                        def chunk(k, b):
                            for t in range(RC):
                                pe.wait_ge(n.hot, (i * NC + k) * RC + t + 1)
                                for g in range(G):
                                    last = pe.matmul(q_z[g // 4][:, g % 4, 0:Z], key_hot[:, t % 2, g * P:g * P + P],
                                                     again[:, b, t, 0:Z], start=False, stop=True, skip_group_check=True)
                                last.then_inc(r_used, 1)

                        chunks(pe, chunk)
                        for h in range(2):
                            pe.matmul(q_z[h][:, 0, 0:Z], zeros_w[:], again[:, 0, 0, 0:Z], start=False, stop=True,
                                      skip_group_check=True).then_inc(n.z, 1)

                    turn(0, 0, 0)

                    def round_n(i, u):
                        turn(i, u, 1)
                        skip(i, 0)
                        if not every:
                            add(i, u, 0)
                        if macro_exists(i + 1):
                            turn(i + 1, (u + 1) % U, 0)
                        skip(i, 1)
                        if every:
                            add_every(i)
                        else:
                            add(i, u, 1)

                    macros(pe, round_n)

                nodes(main, False)
                pe.wait_ge(b_fin, 1)
                with pe.If(pe.value_load(most_i[0:1, 0:1]) > CAP):
                    pe.sem_inc(r_used, CREDIT)
                    nodes(redo, True)


_WEIGHTS = ["W_skip0", "W_skip1", "W_nl0", "W_nl1", "W_fc1", "W_fc2", "W_out_s", "W_out_v"]


def _swap(a, rows, cols):
    import numpy as _np
    n = a.shape[0]
    v = a[:, 64:].reshape(n, rows, cols).transpose(0, 2, 1).reshape(n, rows * cols)
    return _np.ascontiguousarray(_np.concatenate([a[:, :64], v], axis=1))


def layout(inputs):
    import numpy as _np
    et = 125
    arrays = {"x": _swap(_np.asarray(inputs["x"]), 32, 3)}
    for name in ("src", "dst"):
        a = _np.asarray(inputs[name])
        arrays[name] = _np.ascontiguousarray(a.reshape(-1, et).T)
    v = _np.asarray(inputs["edge_attr_3"])
    arrays["edge_vec"] = _np.ascontiguousarray(v.reshape(-1, et, 3).transpose(1, 0, 2))
    arrays["edge_feat_t"] = _np.ascontiguousarray(_np.asarray(inputs["edge_attr_64"]).T)
    for name in _WEIGHTS:
        arrays[name] = _np.ascontiguousarray(_np.asarray(inputs[f"L0_gnn_{name}"]))
    return arrays


def kernel(**inputs):
    import concourse.bacc as _bacc
    from concourse import mybir as _mybir
    from concourse.bass_utils import run_bass_kernel_spmd as _run

    arrays = layout(inputs)
    nc = _bacc.Bacc("TRN2", target_bir_lowering=False, num_devices=1)
    args = [nc.dram_tensor(n, a.shape, _mybir.dt.from_np(a.dtype), kind="ExternalInput").ap()
            for n, a in arrays.items()]
    out = nc.dram_tensor("out_0_dram", arrays["x"].shape, _mybir.dt.float32, kind="ExternalOutput").ap()
    gnn_layer(nc, *args, out)
    r = _run(nc, [arrays], core_ids=[0])
    return _swap(r.results[0]["out_0_dram"], 3, 32)
```

```python
from contextlib import ExitStack

import concourse.bass as bass
from concourse import mybir

ALU = mybir.AluOpType
ACT = mybir.ActivationFunctionType
F32 = mybir.dt.float32
F16 = mybir.dt.float16
BF16 = mybir.dt.bfloat16
I32 = mybir.dt.int32
AX_X = mybir.AxisListType.X

P = 128
EPS = 1e-5


def gnn_layer(nc, x, src, dst, edge_vec, edge_feat_t, w_skip0, w_skip1, w_nl0, w_nl1,
              w_fc1, w_fc2, w_out_s, w_out_v, out):
    N, F = x.shape
    S = w_skip0.shape[0]
    V = w_skip1.shape[0]
    SG = w_skip0.shape[1]
    W = w_fc2.shape[1]
    Z = SG + 3 * V
    assert (S, V, F, SG, W) == (64, 32, 160, 96, 224)

    ET, NT = src.shape
    GE = 4
    NG = NT // GE
    EF = w_fc1.shape[0]
    assert NT % GE == 0 and NT % 8 == 0

    G = 8
    MN = P * G
    NM = -(-N // MN)
    LAST_P = (N - (NM - 1) * MN) // G
    assert N % G == 0
    BPM = G // 2
    NB = NM * BPM
    CAP = P
    MW = 200
    LOCAL, NODE = Z, Z + 1
    TP = 2 * P + 3 * V
    TS = 256

    messages = nc.dram_tensor("messages", (1 + ET * NT, MW), F32).ap()

    with ExitStack() as ctx:
        def sb(name, shape, dt=F32):
            return ctx.enter_context(nc.sbuf_tensor(name, shape, dt))

        def sem(name):
            return ctx.enter_context(nc.semaphore(name))

        ident = sb("ident", [P, P])
        tri_before = sb("tri_before", [ET, ET], BF16)
        tri_rest = sb("tri_rest", [ET, ET], BF16)
        ones_bf = sb("ones_bf", [ET, ET], BF16)
        iota_i = sb("iota_i", [P, 512], I32)
        iota_bin = sb("iota_bin", [P, NB], F16)
        iota_slot = sb("iota_slot", [P, CAP], F16)
        iota_local = sb("iota_local", [P, 2 * P])
        zeros_bf = sb("zeros_bf", [P, NB], BF16)
        neg_half = sb("neg_half", [P, G])
        ones = sb("ones", [P, 1])
        src_i = sb("src_i", [ET, NT], I32)
        dst_i = sb("dst_i", [ET, NT], I32)
        row_i = sb("row_i", [ET, 1], I32)
        tmp_a = sb("tmp_a", [ET, NT], I32)
        tmp_b = sb("tmp_b", [ET, NT], I32)
        bin_of = sb("bin_of", [ET, NT])
        place_of = sb("place_of", [ET, NT, 2])
        tile_no = sb("tile_no", [ET, NT])
        neg_tile = sb("neg_tile", [ET, NT])
        row_no = sb("row_no", [ET, 1])
        vec = sb("vec", [ET, NT, 3])
        vec_sq = sb("vec_sq", [ET, NT, 3])
        vec_d2 = sb("vec_d2", [ET, NT])
        vec_r = sb("vec_r", [ET, NT])
        vec_n = sb("vec_n", [ET, 2, NT])
        hat = sb("hat", [ET, NT, 4])
        slots_i = sb("slots_i", [CAP, NB], I32)
        tab_row = sb("tab_row", [CAP, NB])
        most = sb("most", [ET, 1])
        most_i = sb("most_i", [ET, 1], I32)

        wsk_a = sb("wsk_a", [P, SG + 2 * V])
        wsk_z = sb("wsk_z", [P, 4 * V])
        wnl_a = sb("wnl_a", [P, S + 2 * V])
        wnl_z = sb("wnl_z", [P, 4 * V])
        wfc1 = sb("wfc1", [2 * EF, 2 * EF])
        wfc2 = sb("wfc2", [2 * EF, W])
        wo_a = sb("wo_a", [P, V + SG])
        wo_b = sb("wo_b", [P, SG + 3 * V])
        wo_c = sb("wo_c", [3 * V, 3 * V])

        BR = 8
        bin_hot = sb("bin_hot", [ET, BR, NB], BF16)
        rank_junk = sb("rank_junk", [ET, 2, NB], BF16)
        rank = sb("rank", [ET, BR])
        off_slot = sb("off_slot", [ET, GE, CAP])
        slot_t = sb("slot_t", [ET, GE, CAP], BF16)
        slot_r = sb("slot_r", [ET, GE, CAP], BF16)

        D = 4
        msg = sb("msg", [ET, 2, GE, V + MW])
        hu = sb("hu", [ET, GE, 3, V])
        zeros_w = sb("zeros_w", [ET, P])
        row0 = sb("row0", [1, MW])

        U = 4
        xb = sb("xb", [P, U, G, F])
        n_stat = sb("n_stat", [P, U, G, 6])
        n_sum = sb("n_sum", [P, U, 5, G])
        n_rstd = sb("n_rstd", [P, U, G])
        n_bias = sb("n_bias", [P, U, G])
        nn = sb("nn", [P, 2, 2, F, 4])

        with ExitStack() as msg_ctx:
            def sb_msg(name, shape, dt=F32):
                return msg_ctx.enter_context(nc.sbuf_tensor(name, shape, dt))

            dst_g = sb_msg("dst_g", [ET, D, GE], I32)
            xg = sb_msg("xg", [ET, D, GE, F])
            ef = sb_msg("ef", [2 * EF, 2, 2 * ET])
            e_stat = sb_msg("e_stat", [ET, D, GE, 6])
            e_sum = sb_msg("e_sum", [ET, D, 5, GE])
            e_rstd = sb_msg("e_rstd", [ET, D, GE])
            e_bias = sb_msg("e_bias", [ET, D, GE])
            hn = sb_msg("hn", [ET, 2, F, GE])
            ht = sb_msg("ht", [P, 2, GE * ET])
            hz = sb_msg("hz", [P, 2, ET])
            hid = sb_msg("hid", [2 * EF, 2 * ET])
            w_sb = sb_msg("w_sb", [ET, 2, GE, W])
            tp = sb_msg("tp", [ET, 2, GE, 3 * P])
            xvh = sb_msg("xvh", [ET, GE, 3, V])
            dot = sb_msg("dot", [ET, 2, GE, V])
            w4xv = sb_msg("w4xv", [ET, GE, 3, V])
            cr_a = sb_msg("cr_a", [ET, GE, 3, V])
            cr_b = sb_msg("cr_b", [ET, GE, 3, V])
            tpt = sb_msg("tpt", [P, 2, 3 * ET])

        RC = 10
        NC = NT // RC
        CREDIT = 2 * RC
        again = sb("again", [ET, 2, RC, MW])
        rel = sb("rel", [ET, 2, RC])
        macro_base = sb("macro_base", [ET, 1])
        iota_key = sb("iota_key", [ET, MN])
        key_hot = sb("key_hot", [ET, 2, MN])

        slot_m = sb("slot_m", [P, U, BPM], I32)
        mg = sb("mg", [P, U, BPM, MW])
        hot = sb("hot", [P, 2, BPM, 2 * P])
        off = sb("off", [P, 2 * P])
        nt_a = sb("nt_a", [P, 2, 4 * P])
        nt_z = sb("nt_z", [P, 2, P])
        sg = sb("sg", [P, 2, 4, SG])
        ob = sb("ob", [P, U, G, F])

        s_in = sem("s_in")
        s_w = sem("s_w")
        s_clr = sem("s_clr")
        s_const = sem("s_const")
        s_gp_steps = sem("s_gp_steps")
        s_dve_steps = sem("s_dve_steps")
        s_tab = sem("s_tab")
        s_sqrt = sem("s_sqrt")
        s_wready = sem("s_wready")
        s_row0 = sem("s_row0")
        s_held = sem("s_held")

        b_hot = sem("b_hot")
        b_pre = sem("b_pre")
        b_rank = sem("b_rank")
        b_off = sem("b_off")
        b_slot = sem("b_slot")
        b_row = sem("b_row")
        b_const = sem("b_const")
        b_tab = sem("b_tab")
        b_end = sem("b_end")
        b_rows_sb = sem("b_rows_sb")
        b_most = sem("b_most")
        b_fin = sem("b_fin")

        e_idx = sem("e_idx")
        e_x = [sem(f"e_x{b}") for b in range(D)]
        e_f = [sem("e_f0"), sem("e_f1")]
        e_dot = sem("e_dot")
        e_cross = sem("e_cross")
        e_hu = sem("e_hu")
        e_fix = sem("e_fix")
        e_sums = sem("e_sums")
        e_var = sem("e_var")
        e_pw = sem("e_pw")
        e_ln = sem("e_ln")
        e_norm = sem("e_norm")
        e_t = sem("e_t")
        e_ht = sem("e_ht")
        e_h1 = sem("e_h1")
        e_hid = sem("e_hid")
        e_w = sem("e_w")
        e_wsb = sem("e_wsb")
        e_xs = sem("e_xs")
        e_px = sem("e_px")
        e_w4xv = sem("e_w4xv")
        e_gp = sem("e_gp")
        e_tp = sem("e_tp")
        e_tt = sem("e_tt")
        e_ttsb = sem("e_ttsb")
        e_m = sem("e_m")
        e_msb = sem("e_msb")
        e_st = [sem("e_st0"), sem("e_st1")]

        class Nodes:

            def __init__(self, name):
                self.x = [sem(f"{name}_x{u}") for u in range(U)]
                self.idx = sem(f"{name}_idx")
                self.g = [sem(f"{name}_g{u}") for u in range(U)]
                self.c = sem(f"{name}_c")
                self.var = sem(f"{name}_var")
                self.pw = sem(f"{name}_pw")
                self.ln = sem(f"{name}_ln")
                self.norm = sem(f"{name}_norm")
                self.t = sem(f"{name}_t")
                self.ht = sem(f"{name}_ht")
                self.hot = sem(f"{name}_hot")
                self.off = sem(f"{name}_off")
                self.hot_a = sem(f"{name}_hot_a")
                self.z = sem(f"{name}_z")
                self.sg = sem(f"{name}_sg")
                self.mul = sem(f"{name}_mul")
                self.res = sem(f"{name}_res")
                self.st = [sem(f"{name}_st{u}") for u in range(U)]

        OPEN, ROUNDS = "open", "rounds"
        main = Nodes("n")
        redo = Nodes("r")
        r_iota = sem("r_iota")
        r_key = sem("r_key")
        r_m = [sem("r_m0"), sem("r_m1")]
        r_rel = sem("r_rel")
        r_base = sem("r_base")
        r_used = sem("r_used")

        weight_loads = [(wfc2[0:EF, :], w_fc2), (wfc2[EF:2 * EF, :], w_fc2)]
        for j in range(2):
            part = slice(EF * j, EF * j + EF)
            weight_loads.append((wfc1[part, part], w_fc1))
        weight_loads += [(wo_a[0:S, V:V + SG], w_out_s[0:S, :]), (wo_a[S:2 * S, 0:V], w_out_v[0:S, :]),
                         (wo_b[3 * V:4 * V, 0:SG], w_out_s[S:S + V, :]),
                         (wsk_a[0:S, 0:SG], w_skip0), (wnl_a[0:S, 0:S], w_nl0)]
        for j in range(3):
            part = slice(V * j, V * j + V)
            weight_loads += [(wo_b[part, SG + V * j:SG + V * j + V], w_out_v[S:S + V, :]),
                             (wo_c[part, part], w_out_v[S + V:S + 2 * V, :])]
        for j in range(2):
            rows = slice(S + V * j, S + V * j + V)
            weight_loads += [(wsk_a[rows, SG + V * j:SG + V * j + V], w_skip1),
                             (wnl_a[rows, S + V * j:S + V * j + V], w_nl1)]
        for j in range(4):
            cols = slice(V * j, V * j + V)
            weight_loads += [(wsk_z[j:P:4, cols], w_skip1), (wnl_z[j:P:4, cols], w_nl1)]

        def wait(eng, s, value):
            if not (isinstance(value, int) and value <= 0):
                eng.wait_ge(s, value)

        def earlier(q, b, depth, per):
            return q // depth * per if isinstance(q, int) else (q - b) * (per // depth)

        def edge_tiles(eng, body):
            def round_b(q):
                for k in range(BR):
                    body(q * BR + k, k)

            round_b(0)
            with eng.Fori(1, NT // BR - 1) as q:
                round_b(q)
            round_b(NT // BR - 1)

        def tile_exists(t):
            return not isinstance(t, int) or 0 <= t < NT

        def groups(eng, body):
            loops = (NG - 3 - D) // D
            for q in range(D):
                body(q, q % D)
            with eng.Fori(0, loops) as r:
                for b in range(D):
                    body(D * r + (D + b), b)
            for q in range(D * (loops + 1), NG + 3):
                body(q, q % D)

        def within(q):
            return not isinstance(q, int) or 0 <= q < NG

        def chunks(eng, body):
            with eng.Fori(0, NC // 2) as r:
                body(2 * r, 0)
                body(2 * r + 1, 1)

        def macros(eng, body):
            full = (NM - 4 - U) // U
            for i in range(U):
                body(i, i % U)
            with eng.Fori(0, full) as r:
                for u in range(U):
                    body(U * r + (U + u), u)
            for i in range(U + U * full, NM):
                body(i, i % U)

        def macro_exists(i):
            return not isinstance(i, int) or 0 <= i < NM

        with ExitStack() as psum_ctx:
            def ps(name, shape, dt=F32):
                return psum_ctx.enter_context(nc.psum_tensor(name, shape, dt))

            bank = [ps(f"bank{i}", [P, 1024]) for i in range(4)]

            p_cnt = [bank[0][0:ET, 512 * j:512 * j + NB] for j in range(2)]
            p_tile = bank[1][:, 0:NB]
            p_row = bank[2][:, 0:NB]
            p_t = bank[0][:, 0:GE * ET]
            p_h = p_t[:, 0:2 * ET]
            p_tz = bank[0][:, 512:512 + ET]
            p_w = bank[1][0:ET, :].rearrange("p (t c) -> p t c", c=TS)[:, :, 0:W]
            p_x = bank[2][0:ET, :].rearrange("p (t c) -> p t c", c=TS)[:, :, 0:F]
            p_xs = p_x[:, :, 0:S]
            p_xv = p_x[:, :, S:F].rearrange("p t (i k) -> p t i k", i=3)
            p_m = bank[3][0:ET, 0:2 * (V + Z)].rearrange("p (t c) -> p t c", c=V + Z)
            p_tt = bank[3][:, 512:512 + 3 * ET]
            q_t = [bank[0][:, 0:512], bank[0][:, 512:1024]]
            q_tz = [bank[1][:, 0:P], bank[1][:, 512:512 + P]]
            q_z = [bank[2 + h][:, :].rearrange("p (t c) -> p t c", c=TS) for h in range(2)]

            block = psum_ctx.enter_context(nc.Block())

            @block.sync
            def _(sp):
                sp.dma_start(src_i[:], src).then_inc(s_in, 16)
                sp.dma_start(dst_i[:], dst).then_inc(s_in, 16)
                sp.dma_start(vec[:], edge_vec).then_inc(s_in, 16)
                sp.wait_ge(s_clr, 1)
                for to, of in weight_loads:
                    sp.dma_start(to, of).then_inc(s_w, 16)
                sp.dma_start(messages[0:1, :], row0[:, :]).then_inc(s_row0, 16)

                def store_msgs(p, b):
                    sp.wait_ge(e_fix, p + 1)
                    rows = messages[bass.ds(p * (GE * ET) + 1, GE * ET), :]
                    sp.dma_start(rows.rearrange("(t p) c -> p t c", p=ET), msg[:, b, :, V:V + MW]).then_inc(e_st[b], 16)

                def load_f(q, c):
                    wait(sp, e_h1, q - 1)
                    sp.dma_start(ef[:, c, :], edge_feat_t[bass.ds(q * (2 * EF), 2 * EF), :]).then_inc(e_f[c], 16)

                load_f(0, 0)

                def round_e(q, b):
                    if within(q + 1):
                        load_f(q + 1, 1 - b % 2)
                    if within(q - 3):
                        store_msgs(q - 3, 1 - b % 2)

                def nodes(n, every, parts=(OPEN, ROUNDS)):
                    def load_x(i, u):
                        rows = x[bass.ds(i * MN, MN), :].rearrange("(p g) f -> p g f", g=G)
                        sp.dma_start(xb[:, u, :, :], rows).then_inc(n.x[u], 16)

                    def load_last(u):
                        rows = x[(NM - 1) * MN:N, :].rearrange("(p g) f -> p g f", g=G)
                        sp.dma_start(xb[0:LAST_P, u, :, :], rows).then_inc(n.x[u], 16)

                    def store_o(i, u):
                        sp.wait_ge(n.res, i + 1)
                        if isinstance(i, int) and i == NM - 1:
                            rows = out[(NM - 1) * MN:N, :].rearrange("(p g) f -> p g f", g=G)
                            sp.dma_start(rows, ob[0:LAST_P, u, :, :]).then_inc(n.st[u], 16)
                        else:
                            rows = out[bass.ds(i * MN, MN), :].rearrange("(p g) f -> p g f", g=G)
                            sp.dma_start(rows, ob[:, u, :, :]).then_inc(n.st[u], 16)

                    if OPEN in parts:
                        load_x(0, 0)
                        load_x(1, 1)
                        load_x(2, 2)
                    if ROUNDS not in parts:
                        return

                    def round_n(i, u):
                        if macro_exists(i - 1):
                            store_o(i - 1, (u + 3) % U)
                        if isinstance(i, int) and i + 3 == NM - 1:
                            load_last((u + 3) % U)
                        elif macro_exists(i + 3):
                            load_x(i + 3, (u + 3) % U)
                        if every:
                            def chunk(k, b):
                                sp.wait_ge(r_used, RC * (i * NC + k - 1) + CREDIT)
                                rows = messages[bass.ds(k * (RC * ET) + 1, RC * ET), :]
                                sp.dma_start(again[:, b, :, :], rows.rearrange("(t p) c -> p t c", p=ET)
                                             ).then_inc(r_m[b], 16)

                            chunks(sp, chunk)

                    macros(sp, round_n)
                    store_o(NM - 1, (NM - 1) % U)
                    for u in range(U):
                        sp.wait_ge(n.st[u], 16 * len(range(u, NM, U)))

                nodes(main, False, (OPEN,))
                groups(sp, round_e)
                nodes(main, False, (ROUNDS,))
                sp.wait_ge(b_fin, 1)
                with sp.If(sp.value_load(most_i[0:1, 0:1]) > CAP):
                    nodes(redo, True)

            @block.gpsimd
            def _(pool):
                pool.memset(neg_half[:], -0.5).then_inc(s_const, 1)
                pool.memset(ident[:], 0.0).then_inc(s_gp_steps, 1)
                pool.memset(tri_before[:], 0.0).then_inc(s_gp_steps, 1)
                pool.memset(tri_rest[:], 0.0).then_inc(s_gp_steps, 1)
                pool.iota(iota_i[:], pattern=[[1, 512]], base=0, channel_multiplier=0).then_inc(s_const, 1)
                pool.iota(row_i[:], pattern=[[1, 1]], base=1, channel_multiplier=1).then_inc(s_const, 1)
                pool.wait_ge(s_gp_steps, 3)
                pool.affine_select(out=ident[:], in_=ident[:], compare_op=ALU.not_equal, fill=1.0, base=0,
                                   pattern=[[-1, P]], channel_multiplier=1).then_inc(s_const, 1)
                pool.affine_select(out=tri_before[:], in_=tri_before[:], compare_op=ALU.is_ge, fill=1.0, base=0,
                                   pattern=[[-1, ET]], channel_multiplier=1).then_inc(s_const, 1)
                pool.affine_select(out=tri_rest[:], in_=tri_rest[:], compare_op=ALU.is_gt, fill=1.0, base=0,
                                   pattern=[[1, ET]], channel_multiplier=-1).then_inc(s_const, 1)
                def gathers(q, b):
                    wait(pool, e_norm, q - D + 1)
                    pool.tensor_copy(dst_g[:, b, :], dst_i[:, bass.ds(q * GE, GE)]).then_inc(e_idx, 1)
                    pool.wait_ge(e_idx, q + 1)
                    pool.sem_inc(s_held, 1)
                    for t in range(GE):
                        pool.indirect_dma_start(xg[:, b, t, :], None, x[:, :],
                                                bass.IndirectOffsetOnAxis(ap=dst_g[:, b, t:t + 1], axis=0)
                                                ).then_inc(e_x[b], 16)

                def scales(q, b):
                    pool.wait_ge(e_var, q + 1)
                    pool.tensor_tensor(e_rstd[:, b, :], e_sum[:, b, 4, :], neg_half[0:ET, 0:GE], ALU.pow).then_inc(e_pw, 1)
                    pool.wait_ge(e_pw, q + 1)
                    pool.tensor_tensor(e_bias[:, b, :], e_sum[:, b, 2, :], e_rstd[:, b, :], ALU.mult).then_inc(e_ln, 1)

                pool.wait_ge(s_in, 48)
                gathers(0, 0)
                gathers(1, 1)

                def tile_b(t, k):
                    wait(pool, b_tab, t - GE + 1)
                    pool.wait_ge(b_rank, t + 1)
                    pool.sem_inc(s_held, 1)
                    pool.tensor_scalar(slot_r[:, k % GE, :], iota_slot[0:ET, :], rank[:, k:k + 1], row_no[:, 0:1],
                                       ALU.is_equal, ALU.mult).then_inc(b_row, 1)

                pool.wait_ge(b_const, 1)
                scales(0, 0)
                scales(1, 1)
                edge_tiles(pool, tile_b)
                gathers(2, 2)

                def round_e(q, b):
                    if within(q + 3):
                        gathers(q + 3, (b + 3) % D)
                    if within(q + 2):
                        scales(q + 2, (b + 2) % D)
                    if within(q - 1):
                        p = q - 1
                        h = hat[:, bass.ds(p * GE, GE), :]
                        pool.wait_ge(e_w4xv, p + 1)
                        wait(pool, e_tp, p)
                        pool.tensor_tensor(cr_a[:, :, 0:2, :], w4xv[:, :, 1:3, :],
                                           h[:, :, 2:4].unsqueeze(3).to_broadcast((ET, GE, 2, V)), ALU.mult)
                        pool.tensor_tensor(cr_a[:, :, 2, :], w4xv[:, :, 0, :],
                                           h[:, :, 1:2].to_broadcast((ET, GE, V)), ALU.mult).then_inc(e_gp, 1)
                    if isinstance(q, int) and q == NG:
                        nodes(main, False, (OPEN,))

                def nodes(n, every, parts=(OPEN, ROUNDS)):
                    def fetch(i, u):
                        wait(pool, n.z, 2 * (i - U) + 2)
                        pool.tensor_copy(slot_m[:, u, :], slots_i[:, bass.ds(i * BPM, BPM)]).then_inc(n.idx, 1)
                        pool.wait_ge(n.idx, i + 1)
                        pool.sem_inc(s_held, 1)
                        for k in range(BPM):
                            pool.indirect_dma_start(mg[:, u, k, :], None, messages[:, :],
                                                    bass.IndirectOffsetOnAxis(ap=slot_m[:, u, k:k + 1], axis=0)
                                                    ).then_inc(n.g[u], 16)

                    def ln_n(i, u):
                        pool.wait_ge(n.var, i + 1)
                        pool.tensor_tensor(n_rstd[:, u, :], n_sum[:, u, 4, :], neg_half[:, :], ALU.pow).then_inc(n.pw, 1)
                        pool.wait_ge(n.pw, i + 1)
                        pool.tensor_tensor(n_bias[:, u, :], n_sum[:, u, 2, :], n_rstd[:, u, :], ALU.mult).then_inc(n.ln, 1)

                    if OPEN in parts:
                        ln_n(0, 0)
                        ln_n(1, 1)
                    if ROUNDS not in parts:
                        return
                    if not every:
                        fetch(0, 0)
                        fetch(1, 1)

                    def round_n(i, u):
                        if macro_exists(i + 2):
                            if not every:
                                fetch(i + 2, (u + 2) % U)
                            ln_n(i + 2, (u + 2) % U)

                    macros(pool, round_n)

                groups(pool, round_e)
                pool.wait_ge(b_fin, 1)
                pool.wait_ge(s_row0, 16)
                pool.wait_ge(e_st[0], 16 * (NG // 2))
                pool.wait_ge(e_st[1], 16 * (NG // 2))
                nodes(main, False, (ROUNDS,))
                pool.wait_ge(b_fin, 1)
                with pool.If(pool.value_load(most_i[0:1, 0:1]) > CAP):
                    pool.iota(iota_i[:], pattern=[[1, 4], [G, P]], base=0, channel_multiplier=0).then_inc(r_iota, 1)
                    nodes(redo, True)

            @block.vector
            def _(dve):
                steps = [0]

                def link(ins):
                    steps[0] += 1
                    ins.then_inc(s_dve_steps, 1)
                    dve.wait_ge(s_dve_steps, steps[0])

                for t in (wfc1, wo_a, wo_b, wo_c, wsk_a, wsk_z, wnl_a, wnl_z, row0, zeros_w):
                    dve.memset(t[:], 0.0)
                dve.memset(msg[:, :, :, V + NODE + 1:V + MW], 0.0)
                last = dve.memset(tp[:, :, :, TP:3 * P], 0.0)
                link(last)
                link(dve.memset(row0[:, LOCAL:LOCAL + 1], -1.0))
                dve.memset(ones_bf[:], 1.0)
                dve.memset(ones[:], 1.0)
                dve.memset(zeros_bf[:], 0.0).then_inc(s_clr, 1)
                dve.wait_ge(s_in, 48)
                dve.wait_ge(s_const, 6)
                link(dve.tensor_tensor(vec_sq[:], vec[:], vec[:], ALU.mult))
                link(dve.tensor_tensor(vec_d2[:], vec_sq[:, :, 0], vec_sq[:, :, 1], ALU.add))
                dve.tensor_tensor(vec_d2[:], vec_d2[:], vec_sq[:, :, 2], ALU.add).then_inc(s_tab, 1)
                dve.tensor_copy(iota_bin[:], iota_i[:, 0:NB])
                dve.tensor_copy(iota_slot[:], iota_i[:, 0:CAP])
                dve.tensor_copy(iota_local[:], iota_i[:, 0:2 * P])
                link(dve.tensor_scalar(tmp_a[:], src_i[:], 10, 2, ALU.logical_shift_right, ALU.logical_shift_left))
                link(dve.tensor_scalar(tmp_b[:], src_i[:], 1, BPM - 1, ALU.logical_shift_right, ALU.bitwise_and))
                link(dve.tensor_tensor(bin_of[:], tmp_a[:], tmp_b[:], ALU.add))
                link(dve.tensor_scalar(tmp_a[:], src_i[:], 3, P - 1, ALU.logical_shift_right, ALU.bitwise_and))
                link(dve.tensor_scalar(tmp_b[:], src_i[:], 1, 7, ALU.bitwise_and, ALU.logical_shift_left))
                link(dve.tensor_tensor(place_of[:, :, 0], tmp_a[:], tmp_b[:], ALU.add))
                dve.tensor_copy(place_of[:, :, 1], src_i[:])
                dve.tensor_copy(tile_no[:], iota_i[0:ET, 0:NT])
                link(dve.tensor_copy(row_no[:], row_i[:]))
                def layer_norm(rows, stat, sums, chain, base, done, meanwhile=(None, None)):
                    for t in range(rows.shape[1]):
                        last = dve.bn_stats(stat[:, t, :], rows[:, t, :])
                    last.then_inc(chain, 1)
                    dve.wait_ge(chain, base + 1)
                    dve.tensor_tensor(sums[:, 0, :], stat[:, :, 1], stat[:, :, 4], ALU.subtract)
                    dve.tensor_tensor(sums[:, 1, :], stat[:, :, 2], stat[:, :, 5], ALU.add)
                    dve.tensor_tensor(sums[:, 2, :], stat[:, :, 1], stat[:, :, 4], ALU.add).then_inc(chain, 1)
                    if meanwhile[0]:
                        meanwhile[0]()
                    dve.wait_ge(chain, base + 2)
                    dve.tensor_tensor(sums[:, 3, :], sums[:, 0, :], sums[:, 0, :], ALU.mult)
                    dve.tensor_scalar(sums[:, 1, :], sums[:, 1, :], 1.0 / F, EPS, ALU.mult, ALU.add)
                    dve.tensor_scalar(sums[:, 2, :], sums[:, 2, :], -0.5, None, ALU.mult).then_inc(chain, 1)
                    if meanwhile[1]:
                        meanwhile[1]()
                    dve.wait_ge(chain, base + 3)
                    dve.scalar_tensor_tensor(out=sums[:, 4, :], in0=sums[:, 3, :], scalar=0.25,
                                             in1=sums[:, 1, :], op0=ALU.mult, op1=ALU.add).then_inc(done, 1)

                def stats_e(q, b):
                    dve.wait_ge(e_x[b], earlier(q, b, D, 64) + 64)
                    wait(dve, e_norm, q - D + 1)
                    layer_norm(xg[:, b, :, :], e_stat[:, b, :, :], e_sum[:, b, :, :], e_sums, 3 * q, e_var)

                dve.memset(most[:], 0.0)
                dve.tensor_scalar(neg_tile[:], tile_no[:], -1.0, None, ALU.mult).then_inc(b_const, 1)

                def bins_of(t, k):
                    wait(dve, b_tab, t - BR + 1)
                    dve.tensor_scalar(bin_hot[:, k, :], iota_bin[0:ET, :], bin_of[:, bass.ds(t, 1)], None,
                                      ALU.is_equal).then_inc(b_hot, 1)

                for t in range(4):
                    bins_of(t, t)
                stats_e(0, 0)
                stats_e(1, 1)

                def tile_b(t, k):
                    wait(dve, b_rank, t - 1)
                    dve.wait_ge(b_pre, t + 1)
                    dve.tensor_tensor_reduce(out=rank_junk[:, k % 2, :], in0=bin_hot[:, k, :], in1=p_cnt[k % 2], scale=1.0,
                                             scalar=0.0, op0=ALU.mult, op1=ALU.add,
                                             accum_out=rank[:, k:k + 1]).then_inc(b_rank, 1)
                    if tile_exists(t + 4):
                        bins_of(t + 4, (k + 4) % BR)

                edge_tiles(dve, tile_b)
                dve.wait_ge(b_end, 1)
                dve.reduce_max(most[:], p_cnt[(NT - 1) % 2], AX_X).then_inc(b_most, 1)
                dve.wait_ge(b_most, 1)
                dve.tensor_copy(most_i[:], most[:])
                dve.wait_ge(b_rows_sb, 1)
                dve.scalar_tensor_tensor(out=slots_i[:], in0=p_tile, scalar=float(ET), in1=tab_row[:],
                                         op0=ALU.mult, op1=ALU.add).then_inc(b_fin, 1)
                def products(p, c):
                    w = w_sb[:, c, :, :]
                    h3 = hat[:, bass.ds(p * GE, GE), 0:3].unsqueeze(3)
                    h = hat[:, bass.ds(p * GE, GE), :]
                    dve.wait_ge(e_wsb, p + 1)
                    dve.wait_ge(e_xs, p + 1)
                    wait(dve, e_gp, p)
                    wait(dve, e_tp, p)
                    wait(dve, e_tt, GE * (p - 1))
                    dve.tensor_tensor(w4xv[:], w[:, :, W - V:W].unsqueeze(2).to_broadcast((ET, GE, 3, V)),
                                      p_xv, ALU.mult).then_inc(e_w4xv, 1)
                    dve.tensor_tensor(xvh[:], h3.to_broadcast((ET, GE, 3, V)), p_xv, ALU.mult).then_inc(e_dot, 1)
                    dve.tensor_tensor(tp[:, c, :, 0:2 * S].rearrange("p t (j k) -> p t j k", j=2),
                                      w[:, :, 0:2 * S].rearrange("p t (j k) -> p t j k", j=2),
                                      p_xs.unsqueeze(2).to_broadcast((ET, GE, 2, S)), ALU.mult)
                    dve.tensor_tensor(tp[:, c, :, P:P + 3 * V].rearrange("p t (i k) -> p t i k", i=3),
                                      w[:, :, 2 * S:2 * S + V].unsqueeze(2).to_broadcast((ET, GE, 3, V)),
                                      p_xv, ALU.mult).then_inc(e_px, 1)
                    dve.wait_ge(e_dot, 3 * p + 1)
                    dve.tensor_tensor(dot[:, 0, :, :], xvh[:, :, 0, :], xvh[:, :, 1, :], ALU.add).then_inc(e_dot, 1)
                    dve.wait_ge(e_w4xv, p + 1)
                    dve.tensor_tensor(cr_b[:, :, 0, :], w4xv[:, :, 2, :], h[:, :, 1:2].to_broadcast((ET, GE, V)), ALU.mult)
                    dve.wait_ge(e_dot, 3 * p + 2)
                    dve.tensor_tensor(dot[:, 1, :, :], dot[:, 0, :, :], xvh[:, :, 2, :], ALU.add).then_inc(e_dot, 1)
                    dve.tensor_tensor(cr_b[:, :, 1:3, :], w4xv[:, :, 0:2, :],
                                      h[:, :, 2:4].unsqueeze(3).to_broadcast((ET, GE, 2, V)), ALU.mult).then_inc(e_cross, 1)
                    dve.wait_ge(e_dot, 3 * p + 3)
                    dve.tensor_tensor(tp[:, c, :, P + 3 * V:2 * P], dot[:, 1, :, :],
                                      w[:, :, 2 * S + V:2 * S + 2 * V], ALU.mult)
                    dve.wait_ge(e_cross, p + 1)
                    dve.wait_ge(e_gp, p + 1)
                    dve.tensor_tensor(tp[:, c, :, 2 * P:TP].rearrange("p t (i k) -> p t i k", i=3),
                                      cr_a[:], cr_b[:], ALU.subtract).then_inc(e_tp, 1)

                def complete(p, c):
                    h3 = hat[:, bass.ds(p * GE, GE), 0:3].unsqueeze(3).to_broadcast((ET, GE, 3, V))
                    v = msg[:, c, :, V + SG:V + Z].rearrange("p t (i k) -> p t i k", i=3)
                    dve.wait_ge(e_msb, 2 * p + 2)
                    wait(dve, e_fix, p)
                    dve.tensor_tensor(hu[:], msg[:, c, :, 0:V].unsqueeze(2).to_broadcast((ET, GE, 3, V)), h3,
                                      ALU.mult).then_inc(e_hu, 1)
                    dve.tensor_copy(msg[:, c, :, V + LOCAL:V + NODE + 1], place_of[:, bass.ds(p * GE, GE), :])
                    dve.wait_ge(e_hu, p + 1)
                    dve.tensor_tensor(v, v, hu[:], ALU.add).then_inc(e_fix, 1)

                def round_e(q, b):
                    if within(q + 2):
                        stats_e(q + 2, (b + 2) % D)
                    if within(q - 3):
                        complete(q - 3, (b + 1) % 2)
                    if within(q - 1):
                        products(q - 1, (b + 1) % 2)
                    if isinstance(q, int) and q == NG:
                        nodes(main, False, (OPEN,))

                def nodes(n, every, parts=(OPEN, ROUNDS)):
                    def stats_n(i, u, meanwhile=(None, None)):
                        dve.wait_ge(n.x[u], earlier(i, u, U, 16) + 16)
                        wait(dve, n.norm, 2 * (i - U) + 2)
                        layer_norm(xb[:, u, :, :], n_stat[:, u, :, :], n_sum[:, u, :, :], n.c, 3 * i, n.var,
                                   meanwhile)

                    def hot_n(i, u, bins=range(BPM - 1)):
                        if 0 in bins:
                            dve.wait_ge(n.g[u], earlier(i, u, U, 64) + 64)
                            wait(dve, n.z, 2 * (i - 2) + 2)
                        for k in bins:
                            last = dve.tensor_scalar(hot[:, u % 2, k, :], iota_local[:], mg[:, u, k, LOCAL:LOCAL + 1],
                                                     None, ALU.is_equal)
                        if BPM - 2 in bins:
                            last.then_inc(n.hot, 1)

                    def gate(i, u, h):
                        if h == 0:
                            wait(dve, n.st[u], earlier(i, u, U, 16))
                        dve.wait_ge(n.sg, 2 * i + h + 1)
                        z = q_z[h]
                        o = ob[:, u, 4 * h:4 * h + 4, :]
                        dve.tensor_tensor(o[:, :, 0:S], z[:, :, 0:S], sg[:, h, :, 0:S], ALU.mult)
                        dve.tensor_tensor(o[:, :, S:F].rearrange("p t (i k) -> p t i k", i=3),
                                          z[:, :, SG:Z].rearrange("p t (i k) -> p t i k", i=3),
                                          sg[:, h, :, S:SG].unsqueeze(2).to_broadcast((P, 4, 3, V)),
                                          ALU.mult).then_inc(n.mul, 1)

                    def residual(i, u):
                        dve.wait_ge(n.mul, 2 * i + 2)
                        dve.tensor_tensor(ob[:, u, :, :], ob[:, u, :, :], xb[:, u, :, :], ALU.add).then_inc(n.res, 1)

                    def places(i):
                        def chunk(k, b):
                            c = i * NC + k
                            dve.wait_ge(r_m[b], (c + (2 if b == 0 else 1)) // 2 * 16 if isinstance(c, int)
                                        else (c + (2 if b == 0 else 1)) * 8)
                            dve.tensor_scalar(rel[:, b, :], again[:, b, :, NODE], macro_base[:, :], None,
                                              ALU.subtract).then_inc(r_rel, 1)
                            dve.wait_ge(r_rel, c + 1)
                            for t in range(RC):
                                m = c * RC + t
                                dve.wait_ge(r_used, m - 1 + CREDIT)
                                dve.tensor_scalar(key_hot[:, t % 2, :], iota_key[:], rel[:, b, t:t + 1], None,
                                                  ALU.is_equal).then_inc(n.hot, 1)

                        chunks(dve, chunk)
                        dve.tensor_scalar(macro_base[:], macro_base[:], float(MN), None, ALU.add).then_inc(r_base, 1)
                        dve.wait_ge(r_base, i + 1)

                    if OPEN in parts:
                        stats_n(0, 0)
                        stats_n(1, 1)
                    if ROUNDS not in parts:
                        return
                    if not every:
                        hot_n(0, 0)

                    def round_n(i, u):
                        if macro_exists(i - 1):
                            gate(i - 1, (u + 3) % U, 1)
                            residual(i - 1, (u + 3) % U)
                        if macro_exists(i + 1) and not every:
                            hots = [lambda b=b: hot_n(i + 1, (u + 1) % U, b) for b in (range(0, 2), range(2, BPM - 1))]
                        else:
                            hots = [None, None]
                        if macro_exists(i + 2):
                            stats_n(i + 2, (u + 2) % U, hots)
                        else:
                            for h in hots:
                                if h:
                                    h()
                        if every:
                            places(i)
                        gate(i, u, 0)

                    macros(dve, round_n)
                    gate(NM - 1, (NM - 1) % U, 1)
                    residual(NM - 1, (NM - 1) % U)

                dve.wait_ge(s_sqrt, 1)
                link(dve.reciprocal(vec_r[:], vec_r[:]))
                link(dve.tensor_tensor(vec_n[:, 0, :], vec_r[:], vec_d2[:], ALU.mult))
                link(dve.tensor_tensor(vec_n[:, 1, :], vec_n[:, 0, :], vec_r[:], ALU.mult))
                link(dve.tensor_scalar(vec_n[:, 0, :], vec_n[:, 1, :], -0.5, 1.5, ALU.mult, ALU.add))
                link(dve.tensor_tensor(vec_r[:], vec_r[:], vec_n[:, 0, :], ALU.mult))
                link(dve.tensor_tensor(hat[:, :, 0:3], vec[:], vec_r[:, :].unsqueeze(2).to_broadcast((ET, NT, 3)), ALU.mult))
                dve.tensor_copy(hat[:, :, 3], hat[:, :, 0]).then_inc(s_tab, 1)
                dve.wait_ge(s_tab, 2)
                dve.wait_ge(s_w, 16 * len(weight_loads))
                dve.tensor_scalar(wo_a[0:S, :], wo_a[0:S, :], 1.0 / 32.0, None, ALU.mult)
                dve.tensor_scalar(wo_a[S:2 * S, :], wo_a[S:2 * S, :], 3.0 ** 0.5 / 32.0, None, ALU.mult)
                dve.tensor_scalar(wo_b[:], wo_b[:], 1.0 / 32.0, None, ALU.mult)
                dve.tensor_scalar(wo_c[:], wo_c[:], 1.5 ** 0.5 / 32.0, None, ALU.mult).then_inc(s_wready, 1)
                groups(dve, round_e)
                nodes(main, False, (ROUNDS,))
                dve.wait_ge(b_fin, 1)
                with dve.If(dve.value_load(most_i[0:1, 0:1]) > CAP):
                    dve.wait_ge(r_iota, 1)
                    for g in range(2):
                        dve.tensor_scalar(iota_key[:, 512 * g:512 * g + 512], iota_i[0:ET, :], float(4 * g), None, ALU.add)
                    dve.memset(macro_base[:], 0.0).then_inc(r_key, 1)
                    dve.wait_ge(r_key, 1)
                    nodes(redo, True)

            @block.scalar
            def _(act):
                act.wait_ge(s_tab, 1)
                act.activation(vec_r[:], vec_d2[:], ACT.Sqrt).then_inc(s_sqrt, 1)
                def norm_e(q, b, tiles):
                    act.wait_ge(e_ln, q + 1)
                    wait(act, e_t, q - 1)
                    for t in tiles:
                        last = act.activation(hn[:, b % 2, :, t], xg[:, b, t, :], ACT.Relu,
                                              bias=e_bias[:, b, t:t + 1], scale=e_rstd[:, b, t:t + 1])
                    if GE - 1 in tiles:
                        last.then_inc(e_norm, 1)

                norm_e(0, 0, range(GE))
                act.wait_ge(b_const, 1)

                def slots_of(t, k):
                    act.activation(slot_t[:, k % GE, :], off_slot[:, k % GE, :], ACT.Relu,
                                   bias=tile_no[:, bass.ds(t, 1)], scale=neg_tile[:, bass.ds(t, 1)]).then_inc(b_slot, 1)

                def tile_b(t, k):
                    wait(act, b_tab, t - GE + 1)
                    wait(act, b_off, t)
                    act.wait_ge(b_rank, t + 1)
                    act.activation(off_slot[:, k % GE, :], iota_slot[0:ET, :], ACT.Abs, bias=rank[:, k:k + 1],
                                   scale=-1.0).then_inc(b_off, 1)
                    if tile_exists(t - 1):
                        slots_of(t - 1, (k - 1) % BR)

                edge_tiles(act, tile_b)
                act.wait_ge(b_off, NT)
                slots_of(NT - 1, (NT - 1) % BR)
                act.wait_ge(b_end, 1)
                act.activation(tab_row[:], p_row, ACT.Copy).then_inc(b_rows_sb, 1)

                def round_e(q, b):
                    c = b % 2

                    def take(t):
                        p = q - 2
                        if within(p):
                            act.wait_ge(e_tt, GE * p + t + 1)
                            wait(act, e_m, GE * p + t - 1)
                            act.activation(tpt[:, t % 2, :], p_tt, ACT.Copy).then_inc(e_ttsb, 1)

                    def put(p, c, j):
                        if within(p):
                            act.wait_ge(e_m, GE * p + 2 * j + 2)
                            if j == 0:
                                wait(act, e_st[c], earlier(p, c, 2, 16))
                            act.activation(msg[:, c, 2 * j:2 * j + 2, 0:V + Z], p_m, ACT.Copy).then_inc(e_msb, 1)

                    if within(q):
                        act.wait_ge(e_t, q + 1)
                        wait(act, e_xs, q - 1)
                        act.activation(ht[:, c, :], p_t, ACT.Copy)
                        act.activation(hz[:, c, :], p_tz, ACT.Copy).then_inc(e_ht, 1)
                    put(q - 3, 1 - c, 1)
                    take(0)
                    if within(q):
                        act.wait_ge(e_h1, q + 1)
                        wait(act, e_w, q)
                        act.activation(hid[:], p_h, ACT.Relu).then_inc(e_hid, 1)
                    take(1)
                    if within(q + 1):
                        norm_e(q + 1, (b + 1) % D, range(0, 2))
                    take(2)
                    put(q - 2, c, 0)
                    if within(q + 1):
                        norm_e(q + 1, (b + 1) % D, range(2, 4))
                    take(3)
                    if within(q):
                        act.wait_ge(e_w, q + 1)
                        wait(act, e_tp, q - 1)
                        act.activation(w_sb[:, c, :, :], p_w, ACT.Copy).then_inc(e_wsb, 1)
                    if isinstance(q, int) and q == NG + 1:
                        nodes(main, False, (OPEN,))

                def nodes(n, every, parts=(OPEN, ROUNDS)):
                    def norm(i, u, h):
                        act.wait_ge(n.ln, i + 1)
                        wait(act, n.t, 2 * (i - 2) + h + 1)
                        for g in range(4 * h, 4 * h + 4):
                            last = act.activation(nn[:, u % 2, h, :, g % 4], xb[:, u, g, :], ACT.Relu,
                                                  bias=n_bias[:, u, g:g + 1], scale=n_rstd[:, u, g:g + 1])
                        last.then_inc(n.norm, 1)

                    def evacuate(i, h):
                        act.wait_ge(n.t, 2 * i + h + 1)
                        wait(act, n.z, 2 * i + h - 1)
                        act.activation(nt_a[:, h, :], q_t[h], ACT.Copy)
                        act.activation(nt_z[:, h, :], q_tz[h], ACT.Copy).then_inc(n.ht, 1)

                    def distances(i, u):
                        act.wait_ge(n.g[u], earlier(i, u, U, 64) + 64)
                        wait(act, n.hot_a, i)
                        act.activation(off[:], iota_local[:], ACT.Abs, bias=mg[:, u, BPM - 1, LOCAL:LOCAL + 1],
                                       scale=-1.0).then_inc(n.off, 1)

                    def last_hot(i, u):
                        wait(act, n.z, 2 * (i - 2) + 2)
                        act.wait_ge(n.off, i + 1)
                        act.activation(hot[:, u % 2, BPM - 1, :], off[:], ACT.Relu, bias=ones[:, 0:1],
                                       scale=-1.0).then_inc(n.hot_a, 1)

                    def sigmoids(i, h):
                        act.wait_ge(n.z, 2 * i + h + 1)
                        wait(act, n.mul, 2 * i + h - 1)
                        act.activation(sg[:, h, :, :], q_z[h][:, :, 0:SG], ACT.Sigmoid).then_inc(n.sg, 1)

                    if OPEN in parts:
                        norm(0, 0, 0)
                        norm(0, 0, 1)
                    if ROUNDS not in parts:
                        return
                    evacuate(0, 0)
                    if not every:
                        distances(0, 0)
                        last_hot(0, 0)

                    def round_n(i, u):
                        if macro_exists(i - 1):
                            sigmoids(i - 1, 1)
                        evacuate(i, 1)
                        if macro_exists(i + 1):
                            norm(i + 1, (u + 1) % U, 0)
                            if not every:
                                distances(i + 1, (u + 1) % U)
                        sigmoids(i, 0)
                        if macro_exists(i + 1):
                            if not every:
                                last_hot(i + 1, (u + 1) % U)
                            evacuate(i + 1, 0)
                            norm(i + 1, (u + 1) % U, 1)

                    macros(act, round_n)
                    sigmoids(NM - 1, 1)

                groups(act, round_e)
                nodes(main, False, (ROUNDS,))
                act.wait_ge(b_fin, 1)
                with act.If(act.value_load(most_i[0:1, 0:1]) > CAP):
                    nodes(redo, True)

            @block.tensor
            def _(pe):
                pe.wait_ge(b_hot, 1)
                for o in (p_cnt[0], p_cnt[1], p_tile, p_row):
                    pe.matmul(o, zeros_bf[0:ET, 0:o.shape[0]], zeros_bf[0:ET, :], start=True, stop=False,
                              skip_group_check=True)

                def count(k, tri, of):
                    return pe.matmul(p_cnt[k % 2], tri[:], bin_hot[:, of % BR, :], start=False, stop=False,
                                     skip_group_check=True)

                def table(t, k):
                    pe.wait_ge(b_slot, t + 1)
                    pe.wait_ge(b_row, t + 1)
                    for o, slot in ((p_tile, slot_t), (p_row, slot_r)):
                        last = pe.matmul(o, slot[:, k % GE, :], bin_hot[:, k, :], start=False, stop=False,
                                         skip_group_check=True)
                    last.then_inc(b_tab, 1)

                count(0, tri_before, 0).then_inc(b_pre, 1)
                pe.wait_ge(b_hot, 2)
                count(1, ones_bf, 0)
                count(1, tri_before, 1).then_inc(b_pre, 1)

                def tile_b(t, k):
                    if tile_exists(t + 2):
                        pe.wait_ge(b_hot, t + 3)
                    pe.wait_ge(b_rank, t + 1)
                    count(k, tri_rest, k)
                    if tile_exists(t + 2):
                        count(k, ones_bf, k + 1)
                        count(k, tri_before, k + 2).then_inc(b_pre, 1)
                    if tile_exists(t - 2):
                        table(t - 2, (k - 2) % BR)

                edge_tiles(pe, tile_b)
                table(NT - 2, (NT - 2) % BR)
                table(NT - 1, (NT - 1) % BR)
                for o in (p_cnt[0], p_cnt[1], p_tile, p_row):
                    last = pe.matmul(o, zeros_bf[0:ET, 0:o.shape[0]], zeros_bf[0:ET, :], start=False, stop=True,
                                     skip_group_check=True)
                last.then_inc(b_end, 1)
                pe.wait_ge(b_fin, 1)
                pe.wait_ge(s_w, 16 * len(weight_loads))

                idt = ident[0:ET, 0:ET]

                def turn_rows(q, c):
                    pe.wait_ge(e_norm, q + 1)
                    wait(pe, e_ht, q)
                    wait(pe, e_hid, q)
                    for t in range(GE):
                        pe.transpose(p_t[:, t * ET:(t + 1) * ET], hn[:, c, 0:P, t], idt)
                    pe.transpose(p_tz, hn[:, c, P:F, :], idt).then_inc(e_t, 1)

                turn_rows(0, 0)

                def round_e(q, b):
                    p, c = q - 2, b % 2

                    def turn(t, p=p, c=c):
                        if not within(p):
                            return
                        if t == 0:
                            pe.wait_ge(e_tp, p + 1)
                        wait(pe, e_ttsb, GE * p + t)
                        for i in range(3):
                            last = pe.transpose(p_tt[:, i * ET:(i + 1) * ET], tp[:, c, t, i * P:i * P + P], idt)
                        last.then_inc(e_tt, 1)

                    def project(t):
                        if not within(p):
                            return
                        pe.wait_ge(e_ttsb, GE * p + t + 1)
                        if isinstance(p, int) and p + t == 0:
                            pe.wait_ge(s_wready, 1)
                        if t % 2 == 0:
                            wait(pe, e_msb, 2 * p + t // 2)
                        a = tpt[:, t % 2, :]
                        pe.matmul(p_m[:, t % 2, 0:V + SG], a[:, 0:ET], wo_a[:], start=(t % 2 == 0), stop=True,
                                  skip_group_check=True)
                        pe.matmul(p_m[:, t % 2, V:V + Z], a[:, ET:2 * ET], wo_b[:], start=False, stop=True,
                                  skip_group_check=True)
                        last = pe.matmul(p_m[:, t % 2, V + SG:V + Z], a[0:3 * V, 2 * ET:3 * ET], wo_c[:],
                                         start=False, stop=True, skip_group_check=True)
                        last.then_inc(e_m, 1)

                    def weights(tiles):
                        if not within(q):
                            return
                        if 0 in tiles:
                            pe.wait_ge(e_hid, q + 1)
                            wait(pe, e_wsb, q)
                        for t in tiles:
                            part = slice(EF * (t // 2), EF * (t // 2) + EF)
                            last = pe.matmul(p_w[:, t, :], hid[part, t % 2 * ET:(t % 2 + 1) * ET], wfc2[part, :],
                                             start=True, stop=True)
                        if GE - 1 in tiles:
                            last.then_inc(e_w, 1)

                    if within(q):
                        pe.wait_ge(e_f[c], earlier(q, c, 2, 16) + 16)
                        pe.wait_ge(e_ht, q + 1)
                        pe.matmul(p_h, wfc1[:], ef[:, c, :], start=True, stop=True).then_inc(e_h1, 1)
                    turn(1)
                    project(0)
                    weights((0, 2))
                    turn(2)
                    project(1)
                    weights((1, 3))
                    turn(3)
                    project(2)
                    if within(q + 1):
                        turn_rows(q + 1, 1 - c)
                    project(3)
                    turn(0, p + 1, 1 - c)
                    if within(q):
                        wait(pe, e_px, q)
                        for t in range(GE):
                            pe.matmul(p_x[:, t, 0:P], ht[:, c, t * ET:(t + 1) * ET], wnl_a[:],
                                      start=(t % 2 == 0), stop=True, skip_group_check=True)
                            if t % 2 == 1:
                                j = t // 2
                                last = pe.matmul(p_x[:, 2 * j:2 * j + 2, P:F], hz[:, c, :],
                                                 wnl_z[:, 2 * V * j:2 * V * j + 2 * V],
                                                 start=False, stop=True, skip_group_check=True)
                        last.then_inc(e_xs, 1)

                groups(pe, round_e)
                pe.wait_ge(e_msb, 2 * NG)

                def nodes(n, every):
                    def turn(i, u, h):
                        pe.wait_ge(n.norm, 2 * i + h + 1)
                        wait(pe, n.ht, 2 * i + h - 1)
                        for t in range(4):
                            pe.transpose(q_t[h][:, t * P:(t + 1) * P], nn[:, u % 2, h, 0:P, t], ident[:])
                        pe.transpose(q_tz[h], nn[:, u % 2, h, P:F, :], ident[:]).then_inc(n.t, 1)

                    def skip(i, h):
                        z = q_z[h]
                        pe.wait_ge(n.ht, 2 * i + h + 1)
                        wait(pe, n.mul, 2 * i + h - 1)
                        for t in range(4):
                            pe.matmul(z[:, t, 0:F], nt_a[:, h, t * P:(t + 1) * P], wsk_a[:], start=(t % 2 == 0),
                                      stop=False, skip_group_check=True)
                            if t % 2 == 1:
                                j = t // 2
                                pe.matmul(z[:, 2 * j:2 * j + 2, F:Z], nt_z[:, h, :],
                                          wsk_z[:, 2 * V * j:2 * V * j + 2 * V],
                                          start=False, stop=every, skip_group_check=True)

                    def add(i, u, h):
                        if h == 0:
                            pe.wait_ge(n.hot, i + 1)
                        else:
                            pe.wait_ge(n.hot_a, i + 1)
                        for t in range(4):
                            g = 4 * h + t
                            last = pe.matmul(q_z[h][:, t, 0:Z], hot[:, u % 2, g // 2, (g % 2) * P:(g % 2) * P + P],
                                             mg[:, u, g // 2, 0:Z], start=False, stop=True, skip_group_check=True)
                        last.then_inc(n.z, 1)

                    def add_every(i):
                        def chunk(k, b):
                            for t in range(RC):
                                pe.wait_ge(n.hot, (i * NC + k) * RC + t + 1)
                                for g in range(G):
                                    last = pe.matmul(q_z[g // 4][:, g % 4, 0:Z], key_hot[:, t % 2, g * P:g * P + P],
                                                     again[:, b, t, 0:Z], start=False, stop=True, skip_group_check=True)
                                last.then_inc(r_used, 1)

                        chunks(pe, chunk)
                        for h in range(2):
                            pe.matmul(q_z[h][:, 0, 0:Z], zeros_w[:], again[:, 0, 0, 0:Z], start=False, stop=True,
                                      skip_group_check=True).then_inc(n.z, 1)

                    turn(0, 0, 0)

                    def round_n(i, u):
                        turn(i, u, 1)
                        skip(i, 0)
                        if not every:
                            add(i, u, 0)
                        if macro_exists(i + 1):
                            turn(i + 1, (u + 1) % U, 0)
                        skip(i, 1)
                        if every:
                            add_every(i)
                        else:
                            add(i, u, 1)

                    macros(pe, round_n)

                nodes(main, False)
                pe.wait_ge(b_fin, 1)
                with pe.If(pe.value_load(most_i[0:1, 0:1]) > CAP):
                    pe.sem_inc(r_used, CREDIT)
                    nodes(redo, True)


_WEIGHTS = ["W_skip0", "W_skip1", "W_nl0", "W_nl1", "W_fc1", "W_fc2", "W_out_s", "W_out_v"]


def _swap(a, rows, cols):
    import numpy as _np
    n = a.shape[0]
    v = a[:, 64:].reshape(n, rows, cols).transpose(0, 2, 1).reshape(n, rows * cols)
    return _np.ascontiguousarray(_np.concatenate([a[:, :64], v], axis=1))


def layout(inputs):
    import numpy as _np
    et = 125
    arrays = {"x": _swap(_np.asarray(inputs["x"]), 32, 3)}
    for name in ("src", "dst"):
        a = _np.asarray(inputs[name])
        arrays[name] = _np.ascontiguousarray(a.reshape(-1, et).T)
    v = _np.asarray(inputs["edge_attr_3"])
    arrays["edge_vec"] = _np.ascontiguousarray(v.reshape(-1, et, 3).transpose(1, 0, 2))
    f = _np.asarray(inputs["edge_attr_64"])
    f = f.reshape(-1, 2, 2 * et, f.shape[1]).transpose(0, 1, 3, 2)
    arrays["edge_feat_t"] = _np.ascontiguousarray(f).reshape(-1, 2 * et)
    for name in _WEIGHTS:
        arrays[name] = _np.ascontiguousarray(_np.asarray(inputs[f"L0_gnn_{name}"]))
    return arrays


def kernel(**inputs):
    import concourse.bacc as _bacc
    from concourse import mybir as _mybir
    from concourse.bass_utils import run_bass_kernel_spmd as _run

    arrays = layout(inputs)
    nc = _bacc.Bacc("TRN2", target_bir_lowering=False, num_devices=1)
    args = [nc.dram_tensor(n, a.shape, _mybir.dt.from_np(a.dtype), kind="ExternalInput").ap()
            for n, a in arrays.items()]
    out = nc.dram_tensor("out_0_dram", arrays["x"].shape, _mybir.dt.float32, kind="ExternalOutput").ap()
    gnn_layer(nc, *args, out)
    r = _run(nc, [arrays], core_ids=[0])
    return _swap(r.results[0]["out_0_dram"], 3, 32)
```
